# Optimizing a Trainium2 kernel written in Bass

```python
import numpy as np
import jax
import jax.numpy as jnp

def _softmax(x, axis=-1):
    return jax.nn.softmax(x, axis=axis)

def _gelu(x):
    return jax.nn.gelu(x, approximate=True)

def _silu(x):
    return jax.nn.silu(x)

def _sigmoid(x):
    return jax.nn.sigmoid(x)

def _layernorm(x, axis=-1, eps=1e-05):
    m = jnp.mean(x, axis=axis, keepdims=True)
    v = jnp.var(x, axis=axis, keepdims=True)
    return (x - m) / jnp.sqrt(v + eps)

def _scatter_add(tgt, idx, src, axis=0):
    return tgt.at[idx].add(src)

def _segment_sum(src, seg, n):
    return jax.ops.segment_sum(src, seg, n)
kernel_name = 'mk_decoder_preln_d1_seqx_r8_d9ac2f'

def setup_inputs(seed: int=0):
    np.random.seed(seed)
    _w = jnp.asarray

    def _rec_inputs():
        import jax
        import jax.numpy as jnp
        _rk = jax.random.key(seed)
        x = 7.22e-05 + 1 * jax.random.normal(jax.random.fold_in(_rk, 1), (1, 1024, 128), jnp.float32)
        _lenS = 1024 - jax.random.randint(jax.random.fold_in(_rk, 7), (1,), 0, max(1, 1024 // 4) + 1, jnp.int32)
        _lenS2 = 6404 - jax.random.randint(jax.random.fold_in(_rk, 8), (1,), 0, max(1, 6404 // 4) + 1, jnp.int32)
        _ctx_768P = jax.random.normal(jax.random.fold_in(_rk, 11), (1, 16, 96), jnp.float32)
        _ctx_768c = jax.random.dirichlet(jax.random.fold_in(_rk, 511), 0.3 * jnp.ones((16,), jnp.float32), (1, 6404))
        _ctx_768t = jnp.einsum('bsk,bkd->bsd', _ctx_768c, _ctx_768P)
        _ctx_768t = _ctx_768t * jax.lax.rsqrt(jnp.mean(jnp.square(_ctx_768t)) + 1e-12) * 0.953939
        ctx_768 = -0.000191848 + 0.999787 * (_ctx_768t + 0.3 * jax.random.normal(jax.random.fold_in(_rk, 611), (1, 6404, 96), jnp.float32))
        return (x, ctx_768)
    x, ctx_768 = _rec_inputs()

    def _L0_attn_setup():
        import math
        import jax, jax.numpy as jnp
        import numpy as np
        B, S, D, H = (2, 256, 128, 16)
        HD = D // H
        key = jax.random.key(seed)
        k1, k2, k3 = jax.random.split(key, 3)
        h = jax.random.normal(k1, (B, S, D), dtype=jnp.float32)
        Wqvk = jax.random.normal(k2, (D, 3 * D), dtype=jnp.float32) * (1.0 / math.sqrt(D))
        Wo = jax.random.normal(k3, (D, D), dtype=jnp.float32) * (1.0 / math.sqrt(D))
        return {'h': h, 'Wqvk': Wqvk, 'Wo': Wo}
    _L0_attn_all = _L0_attn_setup()
    _L0_attn_in = {k: v for k, v in _L0_attn_all.items() if k in ('Wqvk', 'Wo')}
    del _L0_attn_all

    def _L0_xattn_setup():
        import jax, jax.numpy as jnp
        import numpy as np
        NUM_HEADS = 16
        CLAMP = 10000.0
        key = jax.random.key(seed)
        ks = jax.random.split(key, 8)
        B, Nq, Nkv, Cq, Ckv = (4, 256, 256, 128, 96)
        s_q = 1.0 / np.sqrt(Cq)
        s_kv = 1.0 / np.sqrt(Ckv)
        return {'query': jax.random.normal(ks[0], (B, Nq, Cq), jnp.float32), 'key_value': jax.random.normal(ks[1], (B, Nkv, Ckv), jnp.float32), 'Wq': jax.random.normal(ks[2], (Cq, Cq), jnp.float32) * s_q, 'bq': jnp.zeros((Cq,), jnp.float32), 'Wk': jax.random.normal(ks[3], (Ckv, Cq), jnp.float32) * s_kv, 'bk': jnp.zeros((Cq,), jnp.float32), 'Wv': jax.random.normal(ks[4], (Ckv, Cq), jnp.float32) * s_kv, 'bv': jnp.zeros((Cq,), jnp.float32), 'Wo': jax.random.normal(ks[5], (Cq, Cq), jnp.float32) * s_q, 'bo': jnp.zeros((Cq,), jnp.float32)}
    _L0_xattn_all = _L0_xattn_setup()
    _L0_xattn_in = {k: v for k, v in _L0_xattn_all.items() if k in ('Wq', 'bq', 'Wk', 'bk', 'Wv', 'bv', 'Wo', 'bo')}
    del _L0_xattn_all

    def _L0_ffn_setup():
        import jax, jax.numpy as jnp
        import numpy as np
        D_MODEL = 128
        D_FF = 512
        NUM_EXPERTS = 8
        TOP_K = 2
        BATCH = 4
        SEQ = 256
        key = jax.random.key(seed)
        ks = jax.random.split(key, 8)
        s = 0.02
        x = jax.random.normal(ks[0], (BATCH, SEQ, D_MODEL), dtype=jnp.float32)
        router_w = jax.random.normal(ks[1], (D_MODEL, NUM_EXPERTS), dtype=jnp.float32) * s
        router_b = jnp.zeros((NUM_EXPERTS,), dtype=jnp.float32)
        W1 = jax.random.normal(ks[2], (NUM_EXPERTS, D_MODEL, D_FF), dtype=jnp.float32) * s
        b1 = jnp.zeros((NUM_EXPERTS, D_FF), dtype=jnp.float32)
        W2 = jax.random.normal(ks[3], (NUM_EXPERTS, D_FF, D_MODEL), dtype=jnp.float32) * s
        b2 = jnp.zeros((NUM_EXPERTS, D_MODEL), dtype=jnp.float32)
        return {'x': x, 'router_w': router_w, 'router_b': router_b, 'W1': W1, 'b1': b1, 'W2': W2, 'b2': b2}
    _L0_ffn_all = _L0_ffn_setup()
    _L0_ffn_in = {k: v for k, v in _L0_ffn_all.items() if k in ('router_w', 'router_b', 'W1', 'b1', 'W2', 'b2')}
    del _L0_ffn_all
    return {'x': x, 'ctx_768': ctx_768, 'L0_attn_Wqvk': _L0_attn_in['Wqvk'], 'L0_attn_Wo': _L0_attn_in['Wo'], 'L0_xattn_Wq': _L0_xattn_in['Wq'], 'L0_xattn_bq': _L0_xattn_in['bq'], 'L0_xattn_Wk': _L0_xattn_in['Wk'], 'L0_xattn_bk': _L0_xattn_in['bk'], 'L0_xattn_Wv': _L0_xattn_in['Wv'], 'L0_xattn_bv': _L0_xattn_in['bv'], 'L0_xattn_Wo': _L0_xattn_in['Wo'], 'L0_xattn_bo': _L0_xattn_in['bo'], 'L0_ffn_router_w': _L0_ffn_in['router_w'], 'L0_ffn_router_b': _L0_ffn_in['router_b'], 'L0_ffn_W1': _L0_ffn_in['W1'], 'L0_ffn_b1': _L0_ffn_in['b1'], 'L0_ffn_W2': _L0_ffn_in['W2'], 'L0_ffn_b2': _L0_ffn_in['b2']}

def reference(x, ctx_768, L0_attn_Wqvk, L0_attn_Wo, L0_xattn_Wq, L0_xattn_bq, L0_xattn_Wk, L0_xattn_bk, L0_xattn_Wv, L0_xattn_bv, L0_xattn_Wo, L0_xattn_bo, L0_ffn_router_w, L0_ffn_router_b, L0_ffn_W1, L0_ffn_b1, L0_ffn_W2, L0_ffn_b2):
    import jax
    import jax.numpy as jnp

    def _L0_attn_ref(h, Wqvk, Wo):
        import math
        import jax, jax.numpy as jnp
        import numpy as np
        B, S, D, H = (2, 256, 128, 16)
        HD = D // H
        b, s, d = h.shape
        qvk = (h @ Wqvk).reshape(b, s, 3, H, HD)
        q, v, k = (qvk[:, :, 0], qvk[:, :, 1], qvk[:, :, 2])
        scores = jnp.einsum('bshi,bthi->bsth', q, k)
        mask = jnp.where(jnp.arange(s)[None, :] > jnp.arange(s)[:, None], jnp.float32(-jnp.inf), jnp.float32(0.0))
        scores = scores + mask[None, :, :, None]
        scores = scores / math.sqrt(d)
        weights = jax.nn.softmax(scores, axis=2)
        wv = jnp.einsum('bsth,bthi->bshi', weights, v).reshape(b, s, d)
        return wv @ Wo

    def _L0_xattn_ref(query, key_value, Wq, bq, Wk, bk, Wv, bv, Wo, bo):
        import jax, jax.numpy as jnp
        import numpy as np
        NUM_HEADS = 16
        CLAMP = 10000.0
        B, Nq, Cq = query.shape
        Nkv = key_value.shape[1]
        H = NUM_HEADS
        D = Cq // H
        scale = D ** (-0.5)
        q = (query @ Wq + bq).reshape(B, Nq, H, D).transpose(0, 2, 1, 3)
        k = (key_value @ Wk + bk).reshape(B, Nkv, H, D).transpose(0, 2, 1, 3)
        v = (key_value @ Wv + bv).reshape(B, Nkv, H, D).transpose(0, 2, 1, 3)
        attn = jnp.einsum('bhqd,bhkd->bhqk', q, k) * scale
        attn = jnp.clip(attn, -CLAMP, CLAMP)
        attn = jax.nn.softmax(attn, axis=-1)
        attn = jnp.where(jnp.any(jnp.isnan(attn)), jnp.asarray(1.0 / Nkv, attn.dtype), attn)
        x = jnp.einsum('bhqk,bhkd->bqhd', attn, v).reshape(B, Nq, Cq)
        return x @ Wo + bo

    def _L0_ffn_ref(x, router_w, router_b, W1, b1, W2, b2):
        import jax, jax.numpy as jnp
        import numpy as np
        D_MODEL = 128
        D_FF = 512
        NUM_EXPERTS = 8
        TOP_K = 2
        BATCH = 4
        SEQ = 256
        logits = jnp.einsum('bsd,de->bse', x, router_w) + router_b
        topk_scores, topk_idx = jax.lax.top_k(logits, TOP_K)
        topk_gates = jax.nn.softmax(topk_scores, axis=-1)
        onehot = jax.nn.one_hot(topk_idx, NUM_EXPERTS, dtype=x.dtype)
        combine = jnp.einsum('bsk,bske->bse', topk_gates, onehot)
        combine_e = jnp.moveaxis(combine, -1, 0)

        def expert_step(acc, params):
            w1, bb1, w2, bb2, c = params
            h = jax.nn.relu(jnp.einsum('bsd,df->bsf', x, w1) + bb1)
            y = jnp.einsum('bsf,fd->bsd', h, w2) + bb2
            return (acc + y * c[..., None], None)
        out, _ = jax.lax.scan(expert_step, jnp.zeros_like(x), (W1, b1, W2, b2, combine_e))
        return out
    x = x + _L0_attn_ref(_layernorm(x, axis=-1), L0_attn_Wqvk, L0_attn_Wo)
    x = x + _L0_xattn_ref(_layernorm(x, axis=-1), ctx_768, L0_xattn_Wq, L0_xattn_bq, L0_xattn_Wk, L0_xattn_bk, L0_xattn_Wv, L0_xattn_bv, L0_xattn_Wo, L0_xattn_bo)
    x = x + _L0_ffn_ref(_layernorm(x, axis=-1), L0_ffn_router_w, L0_ffn_router_b, L0_ffn_W1, L0_ffn_b1, L0_ffn_W2, L0_ffn_b2)
    return x

_drawn_inputs = setup_inputs


def setup_inputs(seed=0):
    import zlib

    import numpy as np

    out = dict(_drawn_inputs(seed))
    spreads = {'L0_xattn_bq': (0.0, 0.454),
     'L0_xattn_bk': (0.0, 0.8),
     'L0_xattn_bv': (0.0, 0.1),
     'L0_xattn_bo': (0.0, 0.1),
     'L0_ffn_router_b': (0.0, 0.32),
     'L0_ffn_b1': (0.0, 0.431),
     'L0_ffn_b2': (0.0, 0.1)}
    factors = {}
    for name, (base, spread) in spreads.items():
        noise = np.random.default_rng([zlib.crc32(name.encode()), seed]).standard_normal(out[name].shape)
        drawn = base * np.exp(spread * noise) if base else spread * noise
        out[name] = jnp.asarray(drawn.astype(out[name].dtype))
    for name, factor in factors.items():
        out[name] = (out[name] * factor).astype(out[name].dtype)
    return out
```

```python
from contextlib import ExitStack

import concourse.bass as bass
from concourse import mybir

F32 = mybir.dt.float32
BF16 = mybir.dt.bfloat16
I32 = mybir.dt.int32
U32 = mybir.dt.uint32
ACT = mybir.ActivationFunctionType
ALU = mybir.AluOpType
AX = mybir.AxisListType

SEQ, D = 1024, 128
H = 16
HD = D // H
KV, C = 6404, 96
P = 128
NBLK = SEQ // P
HALF = 512
NHALF = SEQ // HALF
KT = KV // P
TAIL = KV - KT * P
PARTS = 3
ROWS = PARTS * PARTS * HD
VC = HD + 1
E, FF = 8, 512
NF = FF // P
SELF_SCALE = float(D) ** -0.5
CROSS_SCALE = float(HD) ** -0.5
EPS = 1e-5
MASKED = -1e30
BOUND = 60.0
SLACK = 1.02
FINITE = 1e30
CLAMP = 10000.0
ITERS = H // 2
RING = 4
SRING = 3
CHUNK = 4
NCHUNK = -(-KV // (CHUNK * P))


def cross_plan():
    groups = []
    for half in range(NHALF):
        banks = [[(t, half, 0, HALF, 0)] for t in range(KT)]
        groups += [banks[i:i + 3] for i in range(0, KT, 3)]
    order = [[(t, half) for t in range(KT + 1)] for half in range(NHALF)]
    batches = [(half, order[half][i:i + 4]) for half in range(NHALF) for i in range(0, KT + 1, 4)]
    return groups, batches


def self_plan():
    groups = [
        [[(0, 0, 0, 512, 0)], [(1, 0, 128, 384, 0), (3, 0, 384, 128, 384)],
         [(2, 0, 256, 256, 0), (6, 1, 256, 256, 256)]],
        [[(0, 1, 0, 512, 0)], [(1, 1, 0, 512, 0)], [(2, 1, 0, 512, 0)]],
        [[(3, 1, 0, 512, 0)], [(4, 1, 0, 512, 0)], [(5, 1, 128, 384, 0), (7, 1, 384, 128, 384)]],
    ]
    batches = [(0, [(t, 0) for t in range(4)]), (1, [(t, 1) for t in range(4)]),
               (1, [(t, 1) for t in range(4, 8)])]
    return groups, batches


def decoder_layer(nc, x, ctx, wqvk, wo_s, wq, bq, wk, bk, wv, bv, wo_x, bo, rw, rb, w1, b1, w2, b2, out):
    stack = ExitStack()
    with stack:
        def sb(name, shape, dt=F32):
            return stack.enter_context(nc.sbuf_tensor(name, shape, dt))

        def sem(name):
            return stack.enter_context(nc.semaphore(name))

        x_sb = sb("x_sb", [P, NBLK, D])
        xn = sb("xn", [P, NBLK, D])
        xnT = sb("xnT", [P, SEQ])
        attnT = sb("attnT", [P, SEQ])
        heads_out = sb("heads_out", [32, SEQ // 32, H, HD])
        ctx_region = sb("ctx_region", [P, KT * C])
        ctx_sb = ctx_region[:, :].rearrange("p (t c) -> p t c", c=C)
        w2_sb = ctx_region[:, 0:E * NF * D].rearrange("p (e f d) -> p e f d", e=E, f=NF)
        ctail = sb("ctail", [TAIL, C])
        ctxT_region = sb("ctxT_region", [P, KV])
        ctxT = ctxT_region[0:C + 1, :]
        w1_sb = ctxT_region[:, 0:E * FF].rearrange("p (e f) -> p e f", e=E)
        ctailT = sb("ctailT", [C + 1, H, TAIL])
        kparts = sb("kparts", [P, 2, PARTS, CHUNK * P], BF16)
        ktail = sb("ktail", [P, PARTS, TAIL], BF16)
        ktail_heads = sb("ktail_heads", [P, PARTS, H, TAIL], BF16)
        rest = sb("rest", [P, HALF])
        v_ctx = sb("v_ctx", [P, H, KT + 1, VC])
        v_self = sb("v_self", [P, H, NBLK, VC])
        k_slot = [sb(f"k_slot{s}", [P, KV], BF16) for s in range(2)]
        q_slot = [sb(f"q_slot{s}", [P, SEQ], BF16) for s in range(2)]
        v_slot = [sb(f"v_slot{s}", [P, KT + 1, VC]) for s in range(2)]
        probs = sb("probs", [P, RING, 3, HALF])
        hidden = probs[:, :, 0, :]
        ptail = sb("ptail", [H * TAIL, SEQ])
        turned = sb("turned", [P, NHALF, HALF])
        qparts = sb("qparts", [P, PARTS, SEQ], BF16)
        ksparts = sb("ksparts", [P, PARTS, SEQ], BF16)
        wqvk_sb = sb("wqvk_sb", [D, 3 * D])
        wos_sb = sb("wos_sb", [D, D])
        wq_sb = sb("wq_sb", [D, D])
        wk_sb = sb("wk_sb", [C + 1, D])
        wv_sb = sb("wv_sb", [C + 1, D])
        wox_sb = sb("wox_sb", [D, D])
        bq_sb = sb("bq_sb", [D, 1])
        bo_sb = sb("bo_sb", [1, D])
        rw_sb = sb("rw_sb", [D, E])
        rb_sb = sb("rb_sb", [1, E])
        b1_rows = sb("b1_rows", [E * NF, P])
        b1_sb = sb("b1_sb", [P, E * NF])
        b2_sb = sb("b2_sb", [E, D])
        ident = sb("ident", [P, P])
        identb = sb("identb", [P, P], BF16)
        causal = sb("causal", [P, P], BF16)
        fold = sb("fold", [P, 4, 32])
        head_rows = sb("head_rows", [P, H], BF16)
        tail_rows = sb("tail_rows", [H * TAIL, H])
        one_row = sb("one_row", [1, P])
        spread = v_self[:, :, :, :].rearrange("p h t c -> p (h t c)")[0:E, 0:E * P]\
            .rearrange("p (e q) -> p e q", e=E)
        stats = sb("stats", [P, NBLK, 6])
        mv = sb("mv", [P, NBLK, 2])
        var = sb("var", [P, NBLK])
        rstd = sb("rstd", [P, NBLK])
        newton = sb("newton", [P, NBLK])
        rden = sb("rden", [32, NHALF, HALF // 32])
        squares = probs[:, :, :, :].rearrange("p a b c -> p (a b c)").bitcast(BF16)
        sq_q, sq_k, sq_ctx = squares[:, 0:SEQ], squares[:, SEQ:2 * SEQ], squares[:, 2 * SEQ:2 * SEQ + KV]
        norm_cols = sb("norm_cols", [P, 6])
        verdict = sb("verdict", [1, 6])
        bounded = sb("bounded", [1, 2], I32)
        uneven = sb("uneven", [P, NCHUNK])
        nan_seen = sb("nan_seen", [P, 1])
        chunk_max = sb("chunk_max", [P, NCHUNK])
        neg_max = sb("neg_max", [P, 1])
        rden_gen = sb("rden_gen", [P, 1])
        share = sb("share", [P, 32])
        nan_flag = sb("nan_flag", [32, 1], I32)
        logits = sb("logits", [P, NBLK, E])
        top = sb("top", [P, NBLK, 8])
        top_at = sb("top_at", [P, NBLK, 8], U32)
        top_f = sb("top_f", [P, NBLK, 2])
        gates = sb("gates", [P, NBLK, 2])
        gap = sb("gap", [P, NBLK])
        gap_exp = sb("gap_exp", [P, NBLK])
        expert_no = sb("expert_no", [P, NBLK, E])
        pick = logits
        combine = top
        combineT = attnT[0:E, :]
        yT = turned
        result = xn

        scores = stack.enter_context(nc.psum_tensor("scores", [P, 2, 3, HALF], F32))
        outs = stack.enter_context(nc.psum_tensor("outs", [P, NHALF, HALF], F32))

        def bank(b):
            return scores[:, b // 3, b % 3, :] if b < 6 else outs[:, b - 6, :]

        ks_dram = nc.dram_tensor("ks_parts", (PARTS, D, SEQ), BF16).ap()
        qs_dram = nc.dram_tensor("qs_parts", (PARTS, D, SEQ), BF16).ap()
        kc_dram = nc.dram_tensor("kc_parts", (PARTS, D, KV), BF16).ap()
        qc_dram = nc.dram_tensor("qc_parts", (PARTS, D, SEQ), BF16).ap()

        s = {}
        for name in (
            "x_loaded wself_loaded ctx_loaded0 ctx_loaded1 ctx_loaded2 ctx_loaded3 wctx_loaded wlate_loaded wffn_loaded "
            "ident_made consts_made slots_cleared outs_cleared ones_made dve_step "
            "norm_done normT_ps normT_done qkself_ps qkself_split vself_ps vself_done self_stored "
            "ctxT_ps ctxT_done ctailT_done kctx_ps kctx_first kctx_split vctx_ps vctx_done tail_done "
            "attnT_ps attnT_done proj_ps resid_done qcross_ps qcross_split cross_stored tail_ps tail_exp "
            "b1_ps b1_done router_ps logits_done gap_done gap_exp_done combine_done combineT_ps combineT_done "
            "cb_ps hid_ps hid_relu hid_scaled hid_used yT_done y_ps out_done out_stored "
            "sq_self norms_self sq_ctx norms_ctx sq_cross norms_cross cols_done colsT_ps bounded_made "
            "general_step general_pool kept_all pool_step fold_made spread_made kctx_stored0 kctx_stored1"
        ).split():
            s[name] = sem(name)
        L = []
        for phase in ("self", "cross"):
            L.append({n: sem(f"{phase}_{n}") for n in (
                "qk_done exp_done pv_batches turned0 turned1 folded0 folded1 "
                "kept0 kept1 rden0 rden1 kq_loaded0 kq_loaded1 v_loaded0 v_loaded1").split()})

        G = [{n: sem(f"general{ph}_{n}") for n in (
            "kq v mask round scored copied maxed exped tail turned_ps turned pv dve "
            "uniform nan_ps").split()} for ph in range(2)]
        KQ_DMAS = PARTS + PARTS * PARTS
        plans = [self_plan(), cross_plan()]
        rings = [SRING, RING]
        SC = [SELF_SCALE, CROSS_SCALE]

        def layout(ph):
            groups, batches = plans[ph]
            where = {(t, hf): (g, b, q0, n, col) for g, banks in enumerate(groups)
                     for b, pieces in enumerate(banks) for t, hf, q0, n, col in pieces}
            all_groups = [(hh, g) for hh in range(2) for g in range(len(groups))]
            all_batches = []
            for hh in range(2):
                for hf, members in batches:
                    last = max(where[m][0] for m in members if m in where)
                    all_batches.append((hh, hf, members, hh * len(groups) + last))
            return groups, where, all_groups, all_batches

        def batches_through(ph, g):
            _, where, all_groups, all_batches = layout(ph)
            n = len(plans[ph][0])
            need = 0
            for i, (hh, hf, members, _) in enumerate(all_batches):
                if any(m in where and hh * n + where[m][0] <= g for m in members):
                    need = i + 1
            return need

        keys_of = (SEQ, KV)
        chunks_of = [-(-n // HALF) for n in keys_of]
        tiles_of = (NBLK, KT)

        def choose(eng, ph, fast, general):
            eng.wait_ge(s["bounded_made"], ph + 1)
            within = eng.value_load(bounded[0:1, ph:ph + 1], min_val=0, max_val=1)
            eng.cond(within, fast, general)

        def raw(c, w=HALF):
            return probs[:, c // 3, c % 3, 0:w] if c < 3 * RING else rest[:, 0:w]

        mask_wide = k_slot[1][:, 0:2 * SEQ - P]

        def batches_of(ph):
            return len(layout(ph)[3])

        def half_summed(ph, i, hh, hf):
            last = max(n for n, b in enumerate(layout(ph)[3]) if b[:2] == (hh, hf))
            return i * batches_of(ph) + batches_of(ph) + last + 1

        block = stack.enter_context(nc.Block())

        @block.sync
        def _(sp):
            sp.dma_start(x_sb[:, :, :], x[0].rearrange("(b p) d -> p b d", p=P)).then_inc(s["x_loaded"], 16)
            sp.dma_start(wqvk_sb[:, :], wqvk).then_inc(s["wself_loaded"], 16)
            ctx_keys = ctx[0, 0:KT * P, :].rearrange("(p t) c -> p t c", t=KT)
            sp.dma_start(wk_sb[0:C, :], wk).then_inc(s["wctx_loaded"], 16)
            sp.dma_start(wk_sb[C:C + 1, :], bk.rearrange("(a n) -> a n", a=1)).then_inc(s["wctx_loaded"], 16)
            sp.dma_start(wv_sb[0:C, :], wv).then_inc(s["wctx_loaded"], 16)
            sp.dma_start(wv_sb[C:C + 1, :], bv.rearrange("(a n) -> a n", a=1)).then_inc(s["wctx_loaded"], 16)
            for n, (a, b) in enumerate(((0, 8), (8, 20), (20, 34), (34, KT))):
                sp.dma_start(ctx_sb[:, a:b, :], ctx_keys[:, a:b, :]).then_inc(s[f"ctx_loaded{n}"], 16)
            sp.dma_start(ctail[:, :], ctx[0, KT * P:KV, :]).then_inc(s["wctx_loaded"], 16)
            for dst, src in ((wos_sb[:, :], wo_s), (wq_sb[:, :], wq), (wox_sb[:, :], wo_x),
                             (bq_sb[:, :], bq.rearrange("(n a) -> n a", a=1)),
                             (bo_sb[:, :], bo.rearrange("(a n) -> a n", a=1)),
                             (rw_sb[:, :], rw), (rb_sb[:, :], rb.rearrange("(a n) -> a n", a=1)),
                             (b1_rows[:, :], b1.rearrange("e (f p) -> (e f) p", p=P)),
                             (b2_sb[:, :], b2)):
                sp.dma_start(dst, src).then_inc(s["wlate_loaded"], 16)

            def load_head(ph, slot, head, n_keys, loaded=None):
                loaded = loaded or L[ph][f"kq_loaded{slot}"]
                k_dram, q_dram = ((ks_dram, qs_dram), (kc_dram, qc_dram))[ph]
                for j in range(PARTS):
                    sp.dma_start(k_slot[slot][24 * j:24 * j + 24, 0:n_keys],
                                 k_dram[:, bass.ds(head * HD, HD), :]).then_inc(loaded, 16)
                for j in range(PARTS):
                    for i in range(PARTS):
                        r = 24 * j + 8 * i
                        sp.dma_start(q_slot[slot][r:r + HD, :],
                                     q_dram[j, bass.ds(head * HD, HD), :]).then_inc(loaded, 16)

            def load_next_heads(ph):
                with sp.Fori(0, ITERS - 1) as i:
                    for slot in range(2):
                        sp.wait_ge(L[ph]["qk_done"], (i * 2 + slot + 1) * len(plans[ph][0]))
                        load_head(ph, slot, i * 2 + slot + 2, keys_of[ph])
                sp.wait_ge(L[ph]["qk_done"], (H - 1) * len(plans[ph][0]))
                load_head(ph, 0, 0, keys_of[ph])
                sp.wait_ge(L[ph]["qk_done"], H * len(plans[ph][0]) + 2)

            def load_general(ph):
                for slot in range(2):
                    sp.wait_ge(L[ph][f"kq_loaded{slot}"], 16 * KQ_DMAS)
                with sp.Fori(0, H) as h:
                    sp.wait_ge(G[ph]["round"], h * NBLK + 1)
                    load_head(ph, 0, h, keys_of[ph], G[ph]["kq"])
                sp.wait_ge(G[ph]["round"], H * NBLK + 1)

            sp.wait_ge(s["qkself_split"], 4)
            sp.dma_start(qs_dram.rearrange("i p c -> p i c"), qparts[:, :, :]).then_inc(s["self_stored"], 16)
            sp.dma_start(ks_dram.rearrange("i p c -> p i c"), ksparts[:, :, :]).then_inc(s["self_stored"], 16)
            sp.wait_ge(s["slots_cleared"], 4)
            sp.wait_ge(s["self_stored"], 32)
            for c in range(NCHUNK - 1):
                sp.wait_ge(s["kctx_split"], c + 1)
                sp.dma_start(kc_dram[:, :, c * CHUNK * P:(c + 1) * CHUNK * P].rearrange("i p c -> p i c"),
                             kparts[:, c % 2, :, :]).then_inc(s[f"kctx_stored{c % 2}"], 16)
                if c == 0:
                    for slot in range(2):
                        load_head(0, slot, slot, SEQ)
            c, w = NCHUNK - 1, KV - (NCHUNK - 1) * CHUNK * P
            sp.wait_ge(s["kctx_split"], NCHUNK)
            sp.dma_start(kc_dram[:, :, c * CHUNK * P:KV].rearrange("i p c -> p i c"),
                         kparts[:, c % 2, :, 0:w]).then_inc(s[f"kctx_stored{c % 2}"], 16)
            sp.wait_ge(s["tail_done"], 1)
            sp.wait_ge(s["vctx_done"], NCHUNK)
            sp.dma_start(w1_sb, w1.rearrange("e d f -> d e f")).then_inc(s["wffn_loaded"], 16)
            sp.dma_start(w2_sb, w2.rearrange("e (f p) d -> p e f d", p=P)).then_inc(s["wffn_loaded"], 16)
            choose(sp, 0, lambda: load_next_heads(0), lambda: load_general(0))
            sp.wait_ge(s["qcross_split"], 2)
            sp.dma_start(qc_dram.rearrange("i p c -> p i c"), qparts[:, :, :]).then_inc(s["cross_stored"], 16)
            sp.wait_ge(s["cross_stored"], 16)
            for n in range(2):
                sp.wait_ge(s[f"kctx_stored{n}"], 16 * ((NCHUNK + 1 - n) // 2))
            for slot in range(2):
                load_head(1, slot, slot, KV)
            choose(sp, 1, lambda: load_next_heads(1), lambda: load_general(1))
            out_v = out[0].rearrange("(b p) d -> p b d", p=P)
            for hf in range(NHALF):
                sp.wait_ge(s["out_done"], hf + 1)
                sp.dma_start(out_v[:, 4 * hf:4 * hf + 4, :], result[:, 4 * hf:4 * hf + 4, :]).then_inc(s["out_stored"], 16)
            sp.wait_ge(s["out_stored"], 16 * NHALF)

        @block.gpsimd
        def _(pool):
            made = {}

            def after(ins, what="pool_step"):
                made[what] = made.get(what, 0) + 1
                ins.then_inc(s[what], 1)
                pool.wait_ge(s[what], made[what])

            after(pool.memset(ident[:, :], 0.0))
            after(pool.affine_select(out=ident[:, :], in_=ident[:, :], compare_op=ALU.not_equal, fill=1.0, base=0,
                               pattern=[[-1, P]], channel_multiplier=1), "ident_made")
            after(pool.memset(ctxT_region[C:C + 1, :], 1.0), "ones_made")
            after(pool.memset(ctailT[C:C + 1, :, :], 1.0), "ones_made")
            after(pool.memset(v_self[:, :, :, :], 1.0), "ones_made")
            after(pool.memset(v_ctx[:, :, 0:KT, :], 1.0), "ones_made")
            after(pool.memset(v_ctx[:, :, KT, :], 0.0), "ones_made")
            for slot in range(2):
                after(pool.memset(k_slot[slot][:, :], 0.0), "slots_cleared")
                after(pool.memset(q_slot[slot][:, :], 0.0), "slots_cleared")
            after(pool.memset(identb[:, :], 0.0))
            after(pool.affine_select(out=identb[:, :], in_=identb[:, :], compare_op=ALU.not_equal, fill=1.0, base=0,
                               pattern=[[-1, P]], channel_multiplier=1), "consts_made")
            after(pool.memset(causal[:, :], 0.0))
            after(pool.affine_select(out=causal[:, :], in_=causal[:, :], compare_op=ALU.is_ge, fill=MASKED, base=0,
                               pattern=[[1, P]], channel_multiplier=-1), "consts_made")
            after(pool.memset(fold[:, :, :], 0.0))
            for quad in range(4):
                after(pool.affine_select(out=fold[:, quad:4, :], in_=fold[:, quad:4, :], compare_op=ALU.not_equal,
                                         fill=1.0, base=-32 * quad, pattern=[[0, 4 - quad], [-1, 32]],
                                         channel_multiplier=1), "fold_made")
            for t, width, heads in ((head_rows, HD, P), (tail_rows, TAIL, H * TAIL)):
                after(pool.memset(t[:, :], 1.0))
                after(pool.affine_select(out=t[:, :], in_=t[:, :], compare_op=ALU.is_ge, fill=0.0, base=0,
                                         pattern=[[-width, H]], channel_multiplier=1))
                after(pool.affine_select(out=t[:, :], in_=t[:, :], compare_op=ALU.is_ge, fill=0.0, base=width - 1,
                                   pattern=[[width, H]], channel_multiplier=-1), "consts_made")
            after(pool.memset(one_row[:, :], 1.0), "consts_made")
            after(pool.memset(share[:, :], 1.0 / KV), "consts_made")
            for e in range(E):
                after(pool.memset(expert_no[:, :, e], float(e)), "consts_made")

            v_all = (v_self, v_ctx)
            n_v = (NBLK, KT + 1)

            def load_v(ph):
                for slot in range(2):
                    pool.tensor_copy(v_slot[slot][:, 0:n_v[ph], :], v_all[ph][:, slot, :, :])\
                        .then_inc(L[ph][f"v_loaded{slot}"], 1)
                with pool.Fori(0, ITERS - 1) as i:
                    for slot in range(2):
                        pool.wait_ge(L[ph]["pv_batches"], half_summed(ph, i, slot, NHALF - 1))
                        pool.tensor_copy(v_slot[slot][:, 0:n_v[ph], :],
                                         v_all[ph][:, bass.ds(i * 2 + slot + 2, 1), :, :].rearrange("p a t c -> p (a t) c"))\
                            .then_inc(L[ph][f"v_loaded{slot}"], 1)
                pool.wait_ge(L[ph]["pv_batches"], (ITERS + 1) * batches_of(ph))
                for slot in range(2):
                    pool.wait_ge(L[ph][f"v_loaded{slot}"], ITERS)

            def load_v_general(ph):
                if ph == 0:
                    pool.wait_ge(L[0]["kq_loaded1"], 16 * KQ_DMAS)
                    after(pool.memset(mask_wide, 0.0), "general_pool")
                    pool.affine_select(out=mask_wide, in_=mask_wide, compare_op=ALU.is_ge, fill=MASKED, base=SEQ - P,
                                       pattern=[[-1, 2 * SEQ - P]], channel_multiplier=1).then_inc(G[0]["mask"], 1)
                    pool.wait_ge(G[0]["mask"], 1)
                with pool.Fori(0, H) as h:
                    pool.wait_ge(G[ph]["round"], h * NBLK + 1)
                    pool.tensor_copy(v_slot[0][:, 0:n_v[ph], :],
                                     v_all[ph][:, bass.ds(h, 1), :, :].rearrange("p a t c -> p (a t) c"))\
                        .then_inc(G[ph]["v"], 1)
                pool.wait_ge(G[ph]["round"], H * NBLK + 1)
                pool.wait_ge(G[ph]["v"], H)

            pool.wait_ge(s["vself_done"], 2)
            choose(pool, 0, lambda: load_v(0), lambda: load_v_general(0))
            after(pool.memset(spread[:, :, :], 0.0))
            after(pool.affine_select(out=spread[:, :, :], in_=spread[:, :, :], compare_op=ALU.not_equal, fill=1.0,
                                     base=0, pattern=[[-1, E], [0, P]], channel_multiplier=1), "spread_made")
            pool.wait_ge(s["vctx_done"], NCHUNK)
            pool.wait_ge(s["tail_done"], 1)
            choose(pool, 1, lambda: load_v(1), lambda: load_v_general(1))

        N_CONSTS = 1 + 1 + 2 + 1 + 1 + E

        @block.scalar
        def _(act):
            def evac(dst, src, done, n=1):
                act.activation(dst, src, ACT.Copy).then_inc(done, n)

            def norm_transposed(base):
                for hf in range(NHALF):
                    act.wait_ge(s["normT_ps"], base + hf + 1)
                    evac(xnT[:, hf * HALF:(hf + 1) * HALF], bank(hf), s["normT_done"])

            norm_transposed(0)
            for n in range(4):
                act.wait_ge(s["qkself_ps"], n + 1)
                act.activation((sq_q, sq_k)[n % 2][:, n // 2 * HALF:(n // 2 + 1) * HALF], bank(2 + n), ACT.Square)\
                    .then_inc(s["sq_self"], 1)
            act.wait_ge(s["ones_made"], 5)
            for hf in range(NHALF):
                act.wait_ge(s["vself_ps"], hf + 1)
                evac(v_self[:, :, 4 * hf:4 * hf + 4, 0:HD].rearrange("p h t d -> p t h d"),
                     bank(6 + hf).rearrange("p (t h d) -> p t h d", t=4, h=H), s["vself_done"])

            def ctx_transposed(c):
                w = min(CHUNK * P, KV - c * CHUNK * P)
                act.wait_ge(s["ctxT_ps"], c + 1)
                evac(ctxT_region[0:C, c * CHUNK * P:c * CHUNK * P + w], bank(c % 2)[0:C, 0:w], s["ctxT_done"])

            for c in range(min(2, NCHUNK)):
                ctx_transposed(c)
            for c in range(NCHUNK):
                w = min(CHUNK * P, KV - c * CHUNK * P)
                nt = min(CHUNK, KT - c * CHUNK)
                act.wait_ge(s["kctx_ps"], c + 1)
                if c >= 2:
                    act.wait_ge(s[f"kctx_stored{c % 2}"], 16 * (c // 2))
                act.activation(sq_ctx[:, c * CHUNK * P:c * CHUNK * P + w], bank(2 + c % 2)[:, 0:w], ACT.Square)\
                    .then_inc(s["sq_ctx"], 1)
                evac(kparts[:, c % 2, 0, 0:w], bank(2 + c % 2)[:, 0:w], s["kctx_first"])
                act.wait_ge(s["vctx_ps"], c + 1)
                evac(v_ctx[:, :, c * CHUNK:c * CHUNK + nt, 0:HD].rearrange("p h t d -> p t h d"),
                     bank(4 + c % 2)[:, 0:nt * D].rearrange("p (t h d) -> p t h d", t=nt, h=H), s["vctx_done"])
                if c + 2 < NCHUNK:
                    ctx_transposed(c + 2)

            def exponentials(ph):
                _, _, all_groups, all_batches = layout(ph)
                groups = plans[ph][0]
                n, ring, nb = len(all_groups), rings[ph], len(all_batches)
                if ph == 1:
                    for hf in range(NHALF):
                        act.wait_ge(s["tail_ps"], hf + 1)
                        act.activation(ptail[:, hf * HALF:(hf + 1) * HALF], bank(6 + hf)[0:H * TAIL, :], ACT.Exp,
                                       scale=CROSS_SCALE).then_inc(s["tail_exp"], 1)
                with act.Fori(0, ITERS) as i:
                    for g, (hh, gg) in enumerate(all_groups):
                        nbanks = len(groups[gg])
                        act.wait_ge(L[ph]["qk_done"], i * n + g + 1)
                        if g >= ring:
                            need = nb + batches_through(ph, g - ring)
                        else:
                            need = batches_through(ph, n + g - ring)
                        act.wait_ge(L[ph]["pv_batches"], i * nb + need)
                        act.activation(probs[:, g % ring, 0:nbanks, :], scores[:, g % 2, 0:nbanks, :], ACT.Exp,
                                       scale=SC[ph]).then_inc(L[ph]["exp_done"], 1)

            def general_exponentials(ph):
                nc_, keys = chunks_of[ph], keys_of[ph]
                with act.Fori(0, H) as h:
                    with act.Fori(0, NBLK) as b:
                        n = h * NBLK + b
                        act.wait_ge(G[ph]["maxed"], n + 1)
                        for c in range(nc_):
                            w = min(HALF, keys - c * HALF)
                            act.activation(raw(c, w), raw(c, w), ACT.Exp, bias=neg_max[:, 0:1])\
                                .then_inc(G[ph]["exped"], 1)
                        for c in range(nc_):
                            act.wait_ge(G[ph]["turned_ps"], n * nc_ + c + 1)
                            if c >= 2:
                                act.wait_ge(G[ph]["pv"], n * nc_ + c - 1)
                            w = min(HALF, (tiles_of[ph] * P - c * HALF))
                            ins = act.activation(turned[:, c % 2, 0:w], bank(2 + c % 2)[:, 0:w], ACT.Copy)
                            if ph == 1 and c == nc_ - 1:
                                ins = act.activation(turned[0:H * TAIL, c % 2, w:w + P],
                                                     bank(2 + c % 2)[0:H * TAIL, w:w + P], ACT.Copy)
                            ins.then_inc(G[ph]["turned"], 1)

            choose(act, 0, lambda: exponentials(0), lambda: general_exponentials(0))

            def heads_transposed(base):
                for hf in range(NHALF):
                    act.wait_ge(s["attnT_ps"], base + hf + 1)
                    evac(attnT[:, hf * HALF:(hf + 1) * HALF], bank(hf), s["attnT_done"])

            heads_transposed(0)
            norm_transposed(2)
            for hf in range(NHALF):
                act.wait_ge(s["qcross_ps"], hf + 1)
                act.activation(sq_q[:, hf * HALF:(hf + 1) * HALF], bank(4 + hf), ACT.Square,
                               bias=bq_sb[:, 0:1]).then_inc(s["sq_cross"], 1)
            choose(act, 1, lambda: exponentials(1), lambda: general_exponentials(1))
            heads_transposed(2)
            norm_transposed(4)
            act.wait_ge(s["b1_ps"], 1)
            evac(b1_sb[:, :], bank(5)[:, 0:E * NF], s["b1_done"])
            act.wait_ge(s["gap_done"], 1)
            act.activation(gap_exp[:, :], gap[:, :], ACT.Exp).then_inc(s["gap_exp_done"], 1)
            for hf in range(NHALF):
                act.wait_ge(s["combineT_ps"], hf + 1)
                evac(combineT[:, hf * HALF:(hf + 1) * HALF], bank(3 + hf)[0:E, :], s["combineT_done"])
            act.wait_ge(s["b1_done"], 1)
            for n in range(NHALF * E * NF):
                e, f = n // NF % E, n % NF
                act.wait_ge(s["hid_ps"], n + 1)
                if n >= RING:
                    act.wait_ge(s["hid_used"], n - RING + 1)
                act.activation(hidden[:, n % RING, :], bank(n % 4), ACT.Relu,
                               bias=b1_sb[:, e * NF + f:e * NF + f + 1]).then_inc(s["hid_relu"], 1)
                if n == E * NF + RING or n == NHALF * E * NF - 1:
                    hf = n // (E * NF) if n > E * NF + RING else 0
                    act.wait_ge(s["hid_used"], (hf + 1) * E * NF)
                    evac(yT[:, hf, :], bank(6 + hf), s["yT_done"])

        @block.vector
        def _(dve):
            made = {}

            def step(ins, what="dve_step"):
                made[what] = made.get(what, 0) + 1
                ins.then_inc(s[what], 1)
                dve.wait_ge(s[what], made[what])

            def layernorm():
                for b in range(NBLK):
                    ins = dve.bn_stats(stats[:, b, :], x_sb[:, b, :])
                step(ins)
                for b in range(NBLK):
                    ins = dve.bn_aggr(mv[:, b, :], stats[:, b, :])
                step(ins)
                step(dve.tensor_scalar(var[:, :], mv[:, :, 1], EPS, None, ALU.add))
                step(dve.tensor_scalar(rstd[:, :].bitcast(I32), var[:, :].bitcast(I32), 1, None,
                                       ALU.logical_shift_right))
                step(dve.tensor_scalar(rstd[:, :].bitcast(I32), rstd[:, :].bitcast(I32), -1.0, float(0x5F3759DF),
                                       ALU.mult, ALU.add))
                for _ in range(4):
                    step(dve.tensor_tensor(newton[:, :], rstd[:, :], rstd[:, :], ALU.mult))
                    step(dve.tensor_tensor(newton[:, :], newton[:, :], var[:, :], ALU.mult))
                    step(dve.tensor_scalar(newton[:, :], newton[:, :], -0.5, 1.5, ALU.mult, ALU.add))
                    step(dve.tensor_tensor(rstd[:, :], rstd[:, :], newton[:, :], ALU.mult))
                for b in range(NBLK):
                    ins = dve.tensor_scalar(xn[:, b, :], x_sb[:, b, :], mv[:, b, 0:1], rstd[:, b:b + 1],
                                            ALU.subtract, ALU.mult)
                step(ins, "norm_done")

            def split(src, parts, done, bias=None, first=True):
                w = src.shape[-1]
                r = rest[:, 0:w]
                if bias is None:
                    if first:
                        step(dve.tensor_copy(parts[0], src))
                    step(dve.tensor_tensor(r, src, parts[0], ALU.subtract))
                else:
                    step(dve.tensor_scalar(parts[0], src, bias, None, ALU.add))
                    step(dve.scalar_tensor_tensor(r, src, bias, parts[0], ALU.add, ALU.subtract))
                step(dve.tensor_copy(parts[1], r))
                step(dve.tensor_tensor(parts[2], r, parts[1], ALU.subtract), done)

            dve.memset(outs[:, :, :], 0.0).then_inc(s["outs_cleared"], 1)
            dve.wait_ge(s["x_loaded"], 16)
            layernorm()
            for n in range(4):
                dst = (qparts, ksparts)[n % 2]
                hf = n // 2
                dve.wait_ge(s["sq_self"], n + 1)
                split(bank(2 + n), [dst[:, i, hf * HALF:(hf + 1) * HALF] for i in range(PARTS)], "qkself_split")
            def norm_columns(src, n, at):
                dve.tensor_reduce(norm_cols[:, at:at + 1], src[:, 0:n], AX.X, ALU.max)
                step(dve.tensor_reduce(norm_cols[:, at + 1:at + 2], src[:, 0:n], AX.X, ALU.add), "cols_done")

            def judge(ph):
                limit = (BOUND / (SELF_SCALE, CROSS_SCALE)[ph]) ** 2 / SLACK
                dve.wait_ge(s["colsT_ps"], ph + 1)
                rows = bank(7)[0:1, :].rearrange("p (c n) -> p c n", c=4)
                dve.tensor_reduce(verdict[:, 0:2], rows[:, 0:2, :], AX.X, ALU.max)
                step(dve.tensor_reduce(verdict[:, 2:4], rows[:, 2:4, :], AX.X, ALU.add))
                dve.tensor_scalar(verdict[:, 4:5], verdict[:, 0:1], verdict[:, 1:2], limit, ALU.mult, ALU.is_le)
                step(dve.tensor_scalar(verdict[:, 5:6], verdict[:, 2:3], verdict[:, 3:4], FINITE, ALU.add, ALU.is_le))
                step(dve.tensor_tensor(bounded[:, ph:ph + 1], verdict[:, 4:5], verdict[:, 5:6], ALU.mult), "bounded_made")

            for c in range(NCHUNK):
                w = min(CHUNK * P, KV - c * CHUNK * P)
                if c == 2:
                    dve.wait_ge(s["norms_self"], 1)
                    for n in range(2):
                        norm_columns(bank(6)[:, n * NBLK * H:(n + 1) * NBLK * H], NBLK * H, 2 * n)
                if c == 3:
                    judge(0)
                if c == NCHUNK - 1:
                    dve.wait_ge(s["ones_made"], 2)
                    dve.wait_ge(s["ctxT_done"], NCHUNK)
                    dve.tensor_copy(ctailT[0:C, :, :], ctxT_region[0:C, KT * P:KV].unsqueeze(1)
                                    .to_broadcast([C, H, TAIL])).then_inc(s["ctailT_done"], 1)
                    w0 = KT * P - c * CHUNK * P
                    dve.wait_ge(s["kctx_first"], c + 1)
                    split(bank(2 + c % 2)[:, 0:w], [kparts[:, c % 2, i, 0:w] for i in range(PARTS)],
                          "dve_step", first=False)
                    step(dve.tensor_copy(ktail[:, :, :], kparts[:, c % 2, :, w0:w]), "kctx_split")
                else:
                    dve.wait_ge(s["kctx_first"], c + 1)
                    split(bank(2 + c % 2)[:, 0:w], [kparts[:, c % 2, i, 0:w] for i in range(PARTS)],
                          "kctx_split", first=False)
            dve.wait_ge(s["norms_ctx"], 1)
            norm_columns(bank(6), HALF, 0)
            norm_columns(bank(7), (KT + 1) * H - HALF, 2)
            step(dve.tensor_tensor(norm_cols[:, 2:3], norm_cols[:, 2:3], norm_cols[:, 0:1], ALU.max))
            step(dve.tensor_tensor(norm_cols[:, 3:4], norm_cols[:, 3:4], norm_cols[:, 1:2], ALU.add))
            dve.wait_ge(s["kctx_split"], NCHUNK)
            dve.wait_ge(s["consts_made"], N_CONSTS)
            for i in range(PARTS):
                dve.tensor_tensor(ktail_heads[:, i, :, :], ktail[:, i:i + 1, :].to_broadcast([P, H, TAIL]),
                                  head_rows[:, :].unsqueeze(2).to_broadcast([P, H, TAIL]), ALU.mult)
            dve.wait_ge(s["vctx_ps"], NCHUNK)
            dve.wait_ge(s["vctx_done"], NCHUNK)
            dve.tensor_tensor(v_ctx[0:H * TAIL, :, KT, 0:HD],
                              bank(4 + (NCHUNK - 1) % 2)[0:H * TAIL, 2 * D:3 * D].rearrange("p (h d) -> p h d", h=H),
                              tail_rows[:, :].unsqueeze(2).to_broadcast([H * TAIL, H, HD]), ALU.mult)
            dve.tensor_copy(v_ctx[0:H * TAIL, :, KT, HD], tail_rows[:, :]).then_inc(s["tail_done"], 1)

            def normalise(ph):
                with dve.Fori(0, ITERS) as i:
                    for hh in range(2):
                        for hf in range(NHALF):
                            dve.wait_ge(L[ph]["pv_batches"], half_summed(ph, i, hh, hf))
                            dve.transpose(turned[:, hf, :], outs[:, hf, :]).then_inc(L[ph][f"turned{hf}"], 1)
                        for hf in range(NHALF):
                            dve.wait_ge(L[ph][f"folded{hf}"], i * 2 + hh + 1)
                            got = outs[0:32, hf, 0:HALF // 32 * VC].rearrange("p (c v) -> p c v", v=VC)
                            dve.reciprocal(rden[:, hf, :], got[:, :, HD]).then_inc(L[ph][f"rden{hf}"], 1)
                            dve.wait_ge(L[ph][f"rden{hf}"], i * 2 + hh + 1)
                            nb = HALF // 32
                            dst = heads_out[:, hf * nb:(hf + 1) * nb, bass.ds(i * 2 + hh, 1), :]\
                                .rearrange("p c a d -> p c (a d)")
                            dve.tensor_tensor(dst, got[:, :, 0:HD],
                                              rden[:, hf, :].unsqueeze(2).to_broadcast([32, nb, HD]),
                                              ALU.mult).then_inc(L[ph][f"kept{hf}"], 1)

            def general_rows(ph):
                nc_, keys = chunks_of[ph], keys_of[ph]
                scale = (SELF_SCALE, CROSS_SCALE)[ph]
                steps_in_round = [0]

                def then(ins, n, per_round):
                    steps_in_round[0] += 1
                    ins.then_inc(G[ph]["dve"], 1)
                    dve.wait_ge(G[ph]["dve"], n * per_round + steps_in_round[0])

                per_round = {0: 2, 1: 4}[ph]
                if ph == 1:
                    step(dve.memset(nan_seen[:, :], 0.0), "general_step")
                with dve.Fori(0, H) as h:
                    with dve.Fori(0, NBLK) as b:
                        n = h * NBLK + b
                        steps_in_round[0] = 0
                        if ph == 0:
                            dve.wait_ge(G[0]["mask"], 1)
                        for c in range(nc_):
                            w = min(HALF, keys - c * HALF)
                            dve.wait_ge(G[ph]["scored"], n * nc_ + c + 1)
                            src = bank(c % 2)[:, 0:w]
                            if ph == 0:
                                at = b * -P + ((NBLK - 1) * P + c * HALF)
                                ins = dve.scalar_tensor_tensor(raw(c, w), src, scale, mask_wide[:, bass.ds(at, w)],
                                                               ALU.mult, ALU.add)
                            else:
                                ins = dve.tensor_scalar(raw(c, w), src, scale, None, ALU.mult)
                            ins.then_inc(G[ph]["copied"], 1)
                        dve.wait_ge(G[ph]["copied"], (n + 1) * nc_)
                        if ph == 1:
                            for c in range(nc_):
                                w = min(HALF, keys - c * HALF)
                                ins = dve.tensor_tensor(turned[:, 0, 0:w], raw(c, w), raw(c, w), ALU.not_equal)
                                ins.then_inc(G[ph]["uniform"], 1)
                                dve.wait_ge(G[ph]["uniform"], n * 2 * nc_ + 2 * c + 1)
                                ins = dve.tensor_reduce(uneven[:, c:c + 1], turned[:, 0, 0:w], AX.X, ALU.max)
                                ins.then_inc(G[ph]["uniform"], 1)
                                dve.wait_ge(G[ph]["uniform"], n * 2 * nc_ + 2 * c + 2)
                                ins = dve.tensor_scalar(raw(c, w), raw(c, w), CLAMP, -CLAMP, ALU.min, ALU.max)
                            then(ins, n, per_round)
                            dve.tensor_reduce(turned[:, 1, 0:1], uneven[:, 0:nc_], AX.X, ALU.max)\
                                .then_inc(G[ph]["nan_ps"], 1)
                            dve.wait_ge(G[ph]["nan_ps"], n * 2 + 1)
                            dve.tensor_tensor(nan_seen[:, :], nan_seen[:, :], turned[:, 1, 0:1], ALU.max)\
                                .then_inc(G[ph]["nan_ps"], 1)
                            dve.wait_ge(G[ph]["nan_ps"], n * 2 + 2)
                        for c in range(nc_):
                            w = min(HALF, keys - c * HALF)
                            ins = dve.tensor_reduce(chunk_max[:, c:c + 1], raw(c, w), AX.X, ALU.max)
                        then(ins, n, per_round)
                        then(dve.tensor_reduce(neg_max[:, :], chunk_max[:, 0:nc_], AX.X, ALU.max), n, per_round)
                        dve.tensor_scalar(neg_max[:, :], neg_max[:, :], -1.0, None, ALU.mult).then_inc(G[ph]["maxed"], 1)
                        if ph == 1:
                            dve.wait_ge(G[ph]["exped"], (n + 1) * nc_)
                            at = KV - TAIL - (nc_ - 1) * HALF
                            dve.tensor_copy(top[:, :, :].rearrange("p b e -> p (b e)").rearrange("p (h t) -> p h t", h=H),
                                            raw(nc_ - 1)[:, at:at + TAIL].unsqueeze(1).to_broadcast([P, H, TAIL]))\
                                .then_inc(G[ph]["tail"], 1)
                        dve.wait_ge(G[ph]["pv"], (n + 1) * nc_)
                        ins = dve.reciprocal(rden_gen[:, :], outs[:, 0, HD:HD + 1])
                        if ph == 1:
                            then(ins, n, per_round)
                        else:
                            ins.then_inc(G[ph]["uniform"], 1)
                            dve.wait_ge(G[ph]["uniform"], n + 1)
                        for quad in range(4):
                            dst = heads_out[:, bass.ds(b * 4 + quad, 1), bass.ds(h, 1), :].rearrange("p b a d -> p (b a d)")
                            ins = dve.tensor_scalar(dst, outs[32 * quad:32 * quad + 32, 0, 0:HD],
                                                    rden_gen[32 * quad:32 * quad + 32, :], None, ALU.mult)
                        ins.then_inc(G[ph]["round"], 1)
                dve.wait_ge(G[ph]["round"], H * NBLK + 1)
                if ph == 1:
                    step(dve.tensor_scalar(nan_seen[:, :], nan_seen[:, :], 0.0, None, ALU.is_gt), "general_step")
                    dve.sem_inc(G[ph]["mask"], 1)
                    dve.wait_ge(G[ph]["tail"], H * NBLK + 1)
                    mean = turned[0:32, 0, 0:D]
                    step(dve.tensor_copy(mean, outs[0:32, 1, 0:D]), "general_step")
                    step(dve.tensor_scalar(nan_flag[:, :], outs[0:32, 1, D:D + 1], 0.0, None, ALU.is_gt), "general_step")
                    for b in range(SEQ // 32):
                        ins = dve.copy_predicated(heads_out[:, b, :, :].rearrange("p h d -> p (h d)"),
                                                  nan_flag[:, :].to_broadcast([32, D]), mean)
                    step(ins, "general_step")

            def both_kept(ph):
                step(dve.tensor_copy(verdict[:, 0:1], verdict[:, 1:2]), "kept_all")

            def fast_rows(ph):
                normalise(ph)
                for hf in range(NHALF):
                    dve.wait_ge(L[ph][f"kept{hf}"], H + 1)

            choose(dve, 0, lambda: fast_rows(0), lambda: general_rows(0))
            both_kept(0)

            def residual(base):
                for hf in range(NHALF):
                    dve.wait_ge(s["proj_ps"], base + hf + 1)
                    step(dve.tensor_tensor(x_sb[:, 4 * hf:4 * hf + 4, :],
                                           bank(2 + hf).rearrange("p (b d) -> p b d", d=D),
                                           x_sb[:, 4 * hf:4 * hf + 4, :], ALU.add))

            residual(0)
            layernorm()
            dve.wait_ge(s["wlate_loaded"], 16 * 9)
            for hf in range(NHALF):
                dve.wait_ge(s["sq_cross"], hf + 1)
                if hf == 0:
                    dve.wait_ge(s["self_stored"], 32)
                split(bank(4 + hf), [qparts[:, i, hf * HALF:(hf + 1) * HALF] for i in range(PARTS)],
                      "qcross_split", bias=bq_sb[:, 0:1])
            dve.wait_ge(s["norms_cross"], 1)
            norm_columns(bank(6), NBLK * H, 0)
            judge(1)
            choose(dve, 1, lambda: fast_rows(1), lambda: general_rows(1))
            both_kept(1)
            residual(2)
            layernorm()
            dve.wait_ge(s["router_ps"], 1)
            step(dve.tensor_copy(logits[:, :, :], bank(2)[:, 0:NBLK * E].rearrange("p (b e) -> p b e", e=E)))
            for b in range(NBLK):
                ins = dve.max(top[:, b, :], logits[:, b, :])
            step(ins)
            for b in range(NBLK):
                ins = dve.max_index(top_at[:, b, :], top[:, b, :], logits[:, b, :])
            step(ins)
            dve.tensor_copy(top_f[:, :, :], top_at[:, :, 0:2])
            dve.tensor_tensor(gap[:, :], top[:, :, 1], top[:, :, 0], ALU.subtract).then_inc(s["gap_done"], 1)
            dve.wait_ge(s["gap_exp_done"], 1)
            step(dve.tensor_scalar(gates[:, :, 1], gap_exp[:, :], 1.0, None, ALU.add))
            step(dve.reciprocal(gates[:, :, 0], gates[:, :, 1]))
            step(dve.tensor_tensor(gates[:, :, 1], gap_exp[:, :], gates[:, :, 0], ALU.mult))
            for k, dst in ((0, combine), (1, pick)):
                step(dve.tensor_tensor(dst[:, :, :], expert_no[:, :, :],
                                       top_f[:, :, k:k + 1].to_broadcast([P, NBLK, E]), ALU.is_equal))
                step(dve.tensor_tensor(dst[:, :, :], dst[:, :, :],
                                       gates[:, :, k:k + 1].to_broadcast([P, NBLK, E]), ALU.mult))
            dve.tensor_tensor(combine[:, :, :], combine[:, :, :], pick[:, :, :], ALU.add).then_inc(s["combine_done"], 1)
            for n in range(NHALF * E * NF):
                if n % NF == 0:
                    dve.wait_ge(s["cb_ps"], n // NF + 1)
                dve.wait_ge(s["hid_relu"], n + 1)
                dve.tensor_tensor(hidden[:, n % RING, :], hidden[:, n % RING, :], bank(4 + n // NF % 2),
                                  ALU.mult).then_inc(s["hid_scaled"], 1)
            for hf in range(NHALF):
                dve.wait_ge(s["y_ps"], hf + 1)
                dve.tensor_tensor(result[:, 4 * hf:4 * hf + 4, :], bank(hf).rearrange("p (b d) -> p b d", d=D),
                                  x_sb[:, 4 * hf:4 * hf + 4, :], ALU.add).then_inc(s["out_done"], 1)

        @block.tensor
        def _(pe):
            def transpose_norm(base):
                pe.wait_ge(s["norm_done"], base // 2 + 1)
                for b in range(NBLK):
                    mm = pe.transpose(bank(b // 4)[:, b % 4 * P:(b % 4 + 1) * P], xn[:, b, :], ident[:, :])
                    if b % 4 == 3:
                        mm.then_inc(s["normT_ps"], 1)

            pe.wait_ge(s["ident_made"], 1)
            transpose_norm(0)
            pe.wait_ge(s["wself_loaded"], 16)
            for hf in range(NHALF):
                pe.wait_ge(s["normT_done"], hf + 1)
                for n, col in enumerate((0, 2 * D)):
                    pe.matmul(bank(2 + 2 * hf + n), wqvk_sb[:, col:col + D], xnT[:, hf * HALF:(hf + 1) * HALF],
                              start=True, stop=True).then_inc(s["qkself_ps"], 1)
            pe.wait_ge(s["outs_cleared"], 1)
            for b in range(NBLK):
                mm = pe.matmul(bank(6 + b // 4)[:, b % 4 * D:(b % 4 + 1) * D], xnT[:, b * P:(b + 1) * P],
                               wqvk_sb[:, D:2 * D], start=True, stop=True)
                if b % 4 == 3:
                    mm.then_inc(s["vself_ps"], 1)

            def norms(src, tile, dst, tile_col):
                return pe.matmul(dst[:, tile_col:tile_col + H], src[:, tile:tile + P], head_rows[:, :], start=True, stop=True)

            def turn_columns(ph):
                for n, col in enumerate((0, 2, 1, 3)):
                    mm = pe.transpose(bank(7)[0:1, n * P:(n + 1) * P], norm_cols[:, col:col + 1], ident[:, :])
                mm.then_inc(s["colsT_ps"], 1)

            def transpose_ctx(c):
                if c >= 2:
                    pe.wait_ge(s["ctxT_done"], c - 1)
                for t in range(c * CHUNK, min((c + 1) * CHUNK, KT)):
                    for n, at in enumerate((0, 8, 20, 34)):
                        if t == at:
                            pe.wait_ge(s[f"ctx_loaded{n}"], 16)
                    mm = pe.transpose(bank(c % 2)[0:C, t % CHUNK * P:(t % CHUNK + 1) * P], ctx_sb[:, t, :], ident[:, :])
                if c == NCHUNK - 1:
                    at = KT * P - c * CHUNK * P
                    mm = pe.transpose(bank(c % 2)[0:C, at:at + TAIL], ctail[:, :], ident[0:TAIL, 0:TAIL])
                mm.then_inc(s["ctxT_ps"], 1)

            def project_ctx(c):
                w = min(CHUNK * P, KV - c * CHUNK * P)
                pe.wait_ge(s["ctxT_done"], c + 1)
                if c < 2:
                    pe.wait_ge(s["qkself_split"], 4)
                else:
                    pe.wait_ge(s["kctx_split"], c - 1)
                    pe.wait_ge(s["vctx_done"], c - 1)
                pe.matmul(bank(2 + c % 2)[:, 0:w], wk_sb[:, :], ctxT[:, c * CHUNK * P:c * CHUNK * P + w],
                          start=True, stop=True).then_inc(s["kctx_ps"], 1)
                for t in range(c * CHUNK, min((c + 1) * CHUNK, KT)):
                    mm = pe.matmul(bank(4 + c % 2)[:, t % CHUNK * D:(t % CHUNK + 1) * D], ctxT[:, t * P:(t + 1) * P],
                                   wv_sb[:, :], start=True, stop=True)
                if c == NCHUNK - 1:
                    pe.wait_ge(s["ctailT_done"], 1)
                    mm = pe.matmul(bank(4 + c % 2)[0:H * TAIL, 2 * D:3 * D], ctailT[:, :, :].rearrange("c h t -> c (h t)"),
                                   wv_sb[:, :], start=True, stop=True)
                mm.then_inc(s["vctx_ps"], 1)

            pe.wait_ge(s["normT_done"], 2)
            pe.wait_ge(s["wctx_loaded"], 16 * 5)
            for c in range(min(2, NCHUNK)):
                transpose_ctx(c)
            pe.wait_ge(s["ones_made"], 2)
            for c in range(NCHUNK):
                project_ctx(c)
                if c + 2 < NCHUNK:
                    transpose_ctx(c + 2)
                if c == 1:
                    pe.wait_ge(s["consts_made"], N_CONSTS)
                    pe.wait_ge(s["sq_self"], 4)
                    pe.wait_ge(s["vself_done"], 2)
                    for n, src in enumerate((sq_q, sq_k)):
                        for b in range(NBLK):
                            mm = norms(src, b * P, bank(6), (n * NBLK + b) * H)
                    mm.then_inc(s["norms_self"], 1)
                if c == 3:
                    pe.wait_ge(s["cols_done"], 2)
                    turn_columns(0)
            pe.wait_ge(s["sq_ctx"], NCHUNK)
            pe.wait_ge(s["bounded_made"], 1)
            for t in range(KT + 1):
                mm = norms(sq_ctx, t * P if t < KT else KV - P, bank(6 + t // 32), t % 32 * H)
            mm.then_inc(s["norms_ctx"], 1)

            def attention(ph):
                groups, where, all_groups, all_batches = layout(ph)
                n_groups, nb = len(all_groups), len(all_batches)
                n_tiles = {0: NBLK, 1: KT}[ph]

                def score_group(g, loaded, first_use):
                    hh, gg = all_groups[g]
                    if gg == 0:
                        pe.wait_ge(L[ph][f"kq_loaded{hh}"], loaded)
                    for b, pieces in enumerate(groups[gg]):
                        dst = scores[:, g % 2, b, :]
                        for t, hf, q0, n, col in pieces:
                            diagonal = ph == 0 and hf * HALF + q0 == t * P
                            mm = pe.matmul(dst[:, col:col + n], k_slot[hh][:, t * P:(t + 1) * P],
                                           q_slot[hh][:, hf * HALF + q0:hf * HALF + q0 + n],
                                           start=True, stop=True)
                            if diagonal:
                                mm = pe.matmul(dst[:, col:col + P], identb[:, :], causal[:, :],
                                               start=False, stop=True, skip_group_check=True)
                    mm.then_inc(L[ph]["qk_done"], 1)

                def output_batch(i, b):
                    hh, hf, members, last = all_batches[b]
                    if b == 0 or all_batches[b - 1][1] != hf:
                        pe.wait_ge(L[ph][f"kept{hf}"], i * 2 + hh + 1)
                        if hf == 0:
                            pe.wait_ge(L[ph][f"v_loaded{hh}"], i + 1)
                    for t, _ in members:
                        quad = 32 * (t % 4)
                        if t == n_tiles:
                            mm = pe.matmul(outs[quad:quad + VC, hf, :], v_slot[hh][0:H * TAIL, t, :],
                                           ptail[:, hf * HALF:(hf + 1) * HALF], start=False, stop=True)
                            continue
                        g, bk_, q0, n, col = where[(t, hf)]
                        g += hh * len(groups)
                        final = t + 4 > (n_tiles if ph == 1 else (3 if hf == 0 else NBLK - 1))
                        mm = pe.matmul(outs[quad:quad + VC, hf, q0:q0 + n], v_slot[hh][:, t, :],
                                       probs[:, g % rings[ph], bk_, col:col + n],
                                       start=(t < 4), stop=final)
                    mm.then_inc(L[ph]["pv_batches"], 1)
                    if b + 1 == nb or all_batches[b + 1][1] != hf:
                        ends.append((hh, hf))
                        return True
                    return False

                def fold_half(i, hh, hf):
                    pe.wait_ge(L[ph][f"turned{hf}"], i * 2 + hh + 1)
                    cuts = [(n, 4 * n, 4 * n + 4) for n in range(4)] if (ph, hf) == (0, 0) else [(3, 0, 16)]
                    view = turned[:, hf, :].rearrange("p (c v) -> p c v", v=32)
                    for n, a, b in cuts:
                        mm = pe.matmul(outs[0:32, hf, a * VC:b * VC], fold[:, n, :], view[:, a:b, 0:VC],
                                       start=True, stop=True)
                    mm.then_inc(L[ph][f"folded{hf}"], 1)

                LOAD = 16 * KQ_DMAS
                pe.sem_inc(L[ph]["pv_batches"], nb)
                for hf in range(NHALF):
                    pe.sem_inc(L[ph][f"kept{hf}"], 1)
                if ph == 1:
                    for hf in range(NHALF):
                        for i in range(PARTS):
                            for j in range(PARTS):
                                mm = pe.matmul(bank(6 + hf)[0:H * TAIL, :],
                                               ktail_heads[:, i, :, :].rearrange("p h t -> p (h t)"),
                                               qparts[:, j, hf * HALF:(hf + 1) * HALF],
                                               start=(i + j == 0), stop=(i + j == 2 * PARTS - 2))
                        mm.then_inc(s["tail_ps"], 1)
                score_group(0, LOAD, True)
                score_group(1, LOAD, True)
                if ph == 1:
                    pe.wait_ge(s["tail_exp"], 2)
                ends = []
                with pe.Fori(0, ITERS) as i:
                    done, to_fold = 0, []
                    for g in range(n_groups):
                        nxt = g + 2
                        pe.wait_ge(L[ph]["exp_done"], i * n_groups + g + 1)
                        if nxt < n_groups:
                            score_group(nxt, i * LOAD + LOAD, False)
                        else:
                            score_group(nxt - n_groups, i * LOAD + 2 * LOAD, False)
                        if to_fold and g >= to_fold[0][2]:
                            fold_half(i, to_fold[0][0], to_fold[0][1])
                            to_fold.pop(0)
                        while done < nb and all_batches[done][3] <= g:
                            if output_batch(i, done):
                                hh, hf = ends[-1]
                                to_fold.append((hh, hf, g + (1 if ph == 0 else 2)))
                            done += 1
                    for hh, hf, _ in to_fold:
                        fold_half(i, hh, hf)
                assert done == nb

            def general(ph):
                nc_, keys, n_tiles = chunks_of[ph], keys_of[ph], tiles_of[ph]
                pe.sem_inc(G[ph]["round"], 1)
                with pe.Fori(0, H) as h:
                    with pe.Fori(0, NBLK) as b:
                        n = h * NBLK + b
                        pe.wait_ge(G[ph]["kq"], (h + 1) * 16 * KQ_DMAS)
                        pe.wait_ge(G[ph]["v"], h + 1)
                        pe.wait_ge(G[ph]["round"], n + 1)
                        for c in range(nc_):
                            w = min(HALF, keys - c * HALF)
                            if c >= 2:
                                pe.wait_ge(G[ph]["copied"], n * nc_ + c - 1)
                            pe.matmul(bank(c % 2)[:, 0:w], q_slot[0][:, bass.ds(b * P, P)],
                                      k_slot[0][:, c * HALF:c * HALF + w], start=True, stop=True)\
                                .then_inc(G[ph]["scored"], 1)

                        def turn(c):
                            if ph == 1 and c == nc_ - 1:
                                pe.wait_ge(G[ph]["tail"], n + 1)
                            pe.wait_ge(G[ph]["exped"], n * nc_ + c + 1)
                            if c >= 2:
                                pe.wait_ge(G[ph]["turned"], n * nc_ + c - 1)
                            for t in range(4 * c, min(4 * c + 4, n_tiles)):
                                mm = pe.transpose(bank(2 + c % 2)[:, t % 4 * P:(t % 4 + 1) * P],
                                                  raw(c)[:, t % 4 * P:(t % 4 + 1) * P], ident[:, :])
                            if ph == 1 and c == nc_ - 1:
                                at = n_tiles % 4 * P
                                mm = pe.transpose(bank(2 + c % 2)[0:H * TAIL, at:at + P],
                                                  top[:, :, :].rearrange("p b e -> p (b e)"), ident[:, :])
                            mm.then_inc(G[ph]["turned_ps"], 1)

                        turn(0)
                        turn(1)
                        for c in range(nc_):
                            pe.wait_ge(G[ph]["turned"], n * nc_ + c + 1)
                            for t in range(4 * c, min(4 * c + 4, n_tiles)):
                                last = ph == 0 and t == n_tiles - 1
                                mm = pe.matmul(outs[:, 0, 0:VC], turned[:, c % 2, t % 4 * P:(t % 4 + 1) * P],
                                               v_slot[0][:, t, :], start=(t == 0), stop=last)
                            if ph == 1 and c == nc_ - 1:
                                at = n_tiles % 4 * P
                                mm = pe.matmul(outs[:, 0, 0:VC], turned[0:H * TAIL, c % 2, at:at + P],
                                               v_slot[0][0:H * TAIL, n_tiles, :], start=False, stop=True)
                            mm.then_inc(G[ph]["pv"], 1)
                            if c + 2 < nc_:
                                turn(c + 2)
                pe.wait_ge(G[ph]["round"], H * NBLK + 1)
                if ph == 1:
                    pe.wait_ge(G[ph]["mask"], 1)
                    for t in range(KT):
                        pe.matmul(outs[0:32, 1, 0:D], share[:, :], v_ctx[:, :, t, 0:HD], start=(t == 0), stop=False)
                    pe.matmul(outs[0:32, 1, 0:D], share[0:H * TAIL, :], v_ctx[0:H * TAIL, :, KT, 0:HD],
                              start=False, stop=True)
                    pe.matmul(outs[0:32, 1, D:D + 1], share[:, :], nan_seen[:, :], start=True, stop=True)\
                        .then_inc(G[ph]["tail"], 1)

            pe.wait_ge(s["consts_made"], N_CONSTS)
            pe.wait_ge(s["fold_made"], 4)
            pe.wait_ge(s["kctx_split"], NCHUNK)
            pe.wait_ge(s["vctx_done"], NCHUNK)
            pe.wait_ge(s["tail_done"], 1)
            pe.wait_ge(s["vself_done"], 2)
            choose(pe, 0, lambda: attention(0), lambda: general(0))

            def project_heads(base, w_sb, bias):
                pe.wait_ge(s["kept_all"], base // 2 + 1)
                for hf in range(NHALF):
                    for c in range(HALF // 32):
                        b = hf * (HALF // 32) + c
                        mm = pe.transpose(bank(hf)[:, 32 * c:32 * c + 32],
                                          heads_out[:, b, :, :].rearrange("p h d -> p (h d)"), ident[0:32, 0:32])
                    mm.then_inc(s["attnT_ps"], 1)
                for hf in range(NHALF):
                    pe.wait_ge(s["attnT_done"], base + hf + 1)
                    for b in range(4):
                        dst = bank(2 + hf)[:, b * D:(b + 1) * D]
                        if bias is not None:
                            pe.matmul(dst, one_row[:, :], bias, start=True, stop=False)
                        mm = pe.matmul(dst, attnT[:, hf * HALF + b * P:hf * HALF + (b + 1) * P], w_sb[:, :],
                                       start=bias is None, stop=True)
                    mm.then_inc(s["proj_ps"], 1)

            pe.wait_ge(s["wlate_loaded"], 16 * 9)
            project_heads(0, wos_sb, None)
            transpose_norm(2)
            for hf in range(NHALF):
                pe.wait_ge(s["normT_done"], 2 + hf + 1)
                pe.matmul(bank(4 + hf), wq_sb[:, :], xnT[:, hf * HALF:(hf + 1) * HALF],
                          start=True, stop=True).then_inc(s["qcross_ps"], 1)
            pe.wait_ge(s["qcross_split"], 2)
            pe.wait_ge(s["sq_cross"], 2)
            for b in range(NBLK):
                mm = norms(sq_q, b * P, bank(6), b * H)
            mm.then_inc(s["norms_cross"], 1)
            pe.wait_ge(s["cols_done"], 5)
            turn_columns(1)
            choose(pe, 1, lambda: attention(1), lambda: general(1))
            project_heads(2, wox_sb, bo_sb[:, :])
            transpose_norm(4)
            pe.transpose(bank(5)[:, 0:E * NF], b1_rows[:, :], ident[0:E * NF, 0:E * NF]).then_inc(s["b1_ps"], 1)
            pe.wait_ge(s["normT_done"], 6)
            for b in range(NBLK):
                pe.matmul(bank(2)[:, b * E:(b + 1) * E], one_row[:, :], rb_sb[:, :], start=True, stop=False)
                mm = pe.matmul(bank(2)[:, b * E:(b + 1) * E], xnT[:, b * P:(b + 1) * P], rw_sb[:, :],
                               start=False, stop=True)
            mm.then_inc(s["router_ps"], 1)
            pe.wait_ge(s["combine_done"], 1)
            for b in range(NBLK):
                mm = pe.transpose(bank(3 + b // 4)[0:E, b % 4 * P:(b % 4 + 1) * P], combine[:, b, :], ident[:, :])
                if b % 4 == 3:
                    mm.then_inc(s["combineT_ps"], 1)
            pe.wait_ge(s["wffn_loaded"], 32)
            pe.wait_ge(s["b1_done"], 1)

            def hidden_units(n):
                hf, e, f = n // (E * NF), n // NF % E, n % NF
                if f == 0:
                    if n // NF >= 2:
                        pe.wait_ge(s["hid_scaled"], n - NF)
                    pe.matmul(bank(4 + n // NF % 2), spread[:, e, :], combineT[:, hf * HALF:(hf + 1) * HALF],
                              start=True, stop=True).then_inc(s["cb_ps"], 1)
                if n >= 4:
                    pe.wait_ge(s["hid_relu"], n - 3)
                pe.matmul(bank(n % 4), w1_sb[:, e, f * P:(f + 1) * P], xnT[:, hf * HALF:(hf + 1) * HALF],
                          start=True, stop=True).then_inc(s["hid_ps"], 1)

            def expert_sum(n):
                hf, e, f = n // (E * NF), n // NF % E, n % NF
                first = n % (E * NF) == 0
                if first:
                    pe.matmul(bank(6 + hf), b2_sb[:, :], combineT[:, hf * HALF:(hf + 1) * HALF], start=True, stop=False)
                pe.wait_ge(s["hid_scaled"], n + 1)
                pe.matmul(bank(6 + hf), w2_sb[:, e, f, :], hidden[:, n % RING, :],
                          start=False, stop=n % (E * NF) == E * NF - 1).then_inc(s["hid_used"], 1)

            pe.wait_ge(s["combineT_done"], 2)
            pe.wait_ge(s["spread_made"], 1)
            LAG = 2
            for n in range(NHALF * E * NF + LAG):
                if n < NHALF * E * NF:
                    hidden_units(n)
                if n >= LAG:
                    expert_sum(n - LAG)
            for hf in range(NHALF):
                pe.wait_ge(s["yT_done"], hf + 1)
                for b in range(4):
                    mm = pe.transpose(bank(hf)[:, b * P:(b + 1) * P], yT[:, hf, b * P:(b + 1) * P], ident[:, :])
                mm.then_inc(s["y_ps"], 1)


_NAMES = ["x", "ctx_768", "L0_attn_Wqvk", "L0_attn_Wo", "L0_xattn_Wq", "L0_xattn_bq", "L0_xattn_Wk", "L0_xattn_bk",
          "L0_xattn_Wv", "L0_xattn_bv", "L0_xattn_Wo", "L0_xattn_bo", "L0_ffn_router_w", "L0_ffn_router_b",
          "L0_ffn_W1", "L0_ffn_b1", "L0_ffn_W2", "L0_ffn_b2"]


def kernel(**inputs):
    import numpy as np
    import concourse.bacc as bacc
    from concourse.bass_utils import run_bass_kernel_spmd as run

    nc = bacc.Bacc("TRN2", target_bir_lowering=False, num_devices=1)
    arrays, args = {}, []
    for name in _NAMES:
        a = np.ascontiguousarray(inputs[name])
        arrays[f"in_{name}"] = a
        args.append(nc.dram_tensor(f"in_{name}", a.shape, mybir.dt.from_np(a.dtype), kind="ExternalInput").ap())
    out = nc.dram_tensor("out", (1, SEQ, D), F32, kind="ExternalOutput").ap()
    decoder_layer(nc, *args, out)
    r = run(nc, [arrays], core_ids=[0])
    return r.results[0]["out"]
```

```python
from contextlib import ExitStack

import concourse.bass as bass
from concourse import mybir

F32 = mybir.dt.float32
BF16 = mybir.dt.bfloat16
I32 = mybir.dt.int32
U32 = mybir.dt.uint32
ACT = mybir.ActivationFunctionType
ALU = mybir.AluOpType
AX = mybir.AxisListType

SEQ, D = 1024, 128
H = 16
HD = D // H
KV, C = 6404, 96
P = 128
NBLK = SEQ // P
HALF = 512
NHALF = SEQ // HALF
KT = KV // P
TAIL = KV - KT * P
PARTS = 3
ROWS = PARTS * PARTS * HD
VC = HD + 1
E, FF = 8, 512
NF = FF // P
SELF_SCALE = float(D) ** -0.5
CROSS_SCALE = float(HD) ** -0.5
EPS = 1e-5
MASKED = -1e30
BOUND = 60.0
SLACK = 1.02
FINITE = 1e30
CLAMP = 10000.0
ITERS = H // 2
RING = 4
SRING = 3
LAG = 2
CHUNK = 4
KRING = 4
NCHUNK = -(-KV // (CHUNK * P))


def cross_plan():
    groups = []
    for half in range(NHALF):
        banks = [[(t, half, 0, HALF, 0)] for t in range(KT)]
        groups += [banks[i:i + 3] for i in range(0, KT, 3)]
    order = [[(t, half) for t in range(KT + 1)] for half in range(NHALF)]
    batches = [(half, order[half][i:i + 4]) for half in range(NHALF) for i in range(0, KT + 1, 4)]
    return groups, batches


def self_plan():
    groups = [
        [[(0, 1, 0, 512, 0)], [(1, 1, 0, 512, 0)], [(2, 1, 0, 512, 0)]],
        [[(3, 1, 0, 512, 0)], [(4, 1, 0, 512, 0)], [(5, 1, 128, 384, 0), (7, 1, 384, 128, 384)]],
        [[(6, 1, 256, 256, 256), (2, 0, 256, 256, 0)], [(0, 0, 0, 512, 0)],
         [(1, 0, 128, 384, 0), (3, 0, 384, 128, 384)]],
    ]
    batches = [(1, [(t, 1) for t in range(4)]), (1, [(t, 1) for t in range(4, 8)]),
               (0, [(t, 0) for t in range(4)])]
    return groups, batches


def decoder_layer(nc, x, ctx, wqvk, wo_s, wq, bq, wk, bk, wv, bv, wo_x, bo, rw, rb, w1, b1, w2, b2, out):
    stack = ExitStack()
    with stack:
        def sb(name, shape, dt=F32):
            return stack.enter_context(nc.sbuf_tensor(name, shape, dt))

        def sem(name):
            return stack.enter_context(nc.semaphore(name))

        x_sb = sb("x_sb", [P, NBLK, D])
        xn = sb("xn", [P, NBLK, D])
        xnT = sb("xnT", [P, SEQ])
        attnT = sb("attnT", [P, SEQ])
        heads_out = sb("heads_out", [32, SEQ // 32, H, HD])
        ctx_region = sb("ctx_region", [P, KT * C])
        ctx_sb = ctx_region[:, :].rearrange("p (t c) -> p t c", c=C)
        w2_sb = ctx_region[:, 0:E * NF * D].rearrange("p (e f d) -> p e f d", e=E, f=NF)
        ctail = sb("ctail", [TAIL, C])
        ctxT_region = sb("ctxT_region", [P, KV])
        ctxT = ctxT_region[0:C + 1, :]
        w1_sb = ctxT_region[:, 0:E * FF].rearrange("p (e f) -> p e f", e=E)
        ctailT = sb("ctailT", [C + 1, H, TAIL])
        kparts_ab = sb("kparts_ab", [P, 2, PARTS, CHUNK * P], BF16)
        ktail = sb("ktail", [P, PARTS, TAIL], BF16)
        ktail_heads = sb("ktail_heads", [P, PARTS, H, TAIL], BF16)
        rest = sb("rest", [P, HALF])
        v_ctx = sb("v_ctx", [P, H, KT + 1, VC])
        v_self = sb("v_self", [P, H, NBLK, VC])
        k_slot = [sb(f"k_slot{s}", [P, KV], BF16) for s in range(2)]
        q_slot = [sb(f"q_slot{s}", [P, SEQ], BF16) for s in range(2)]
        v_slot = [sb(f"v_slot{s}", [P, KT + 1, VC]) for s in range(2)]
        probs = sb("probs", [P, RING, 3, HALF])
        gate_rows = probs[:, 0:2, 1, :]
        hidden = probs[:, :, 0, :]
        ptail = sb("ptail", [H * TAIL, SEQ])
        turned = sb("turned", [P, NHALF, HALF])
        qparts = sb("qparts", [P, PARTS, SEQ], BF16)
        ksparts = sb("ksparts", [P, PARTS, SEQ], BF16)
        wqvk_sb = sb("wqvk_sb", [D, 3 * D])
        wos_sb = sb("wos_sb", [D, D])
        wq_sb = sb("wq_sb", [D, D])
        wk_sb = sb("wk_sb", [C + 1, D])
        wv_sb = sb("wv_sb", [C + 1, D])
        wox_sb = sb("wox_sb", [D, D])
        bq_sb = sb("bq_sb", [D, 1])
        bo_rows = sb("bo_rows", [P, D])
        rw_sb = sb("rw_sb", [D, E])
        rb_sb = sb("rb_sb", [E, 1])
        b1_rows = sb("b1_rows", [E * NF, P])
        b1_sb = sb("b1_sb", [P, E * NF])
        b2_sb = sb("b2_sb", [E, D])
        b2T_sb = sb("b2T_sb", [D, E])
        ident = sb("ident", [P, P])
        identb = sb("identb", [P, P], BF16)
        causal = sb("causal", [P, P], BF16)
        fold = sb("fold", [P, 4, 32])
        head_rows = sb("head_rows", [P, H], BF16)
        tail_rows = sb("tail_rows", [H * TAIL, H])
        spread = v_self[:, :, :, :].rearrange("p h t c -> p (h t c)")[0:E, 0:E * P]\
            .rearrange("p (e q) -> p e q", e=E)
        stats = sb("stats", [P, NBLK, 6])
        mv = sb("mv", [P, NBLK, 2])
        var = sb("var", [P, NBLK])
        rstd = sb("rstd", [P, NBLK])
        newton = sb("newton", [P, NBLK])
        rden = sb("rden", [32, NHALF, HALF // 32])
        squares = probs[:, :, :, :].rearrange("p a b c -> p (a b c)").bitcast(BF16)
        kparts = squares[:, 2 * SEQ + KV:2 * SEQ + KV + 2 * PARTS * CHUNK * P]\
            .rearrange("p (r i c) -> p r i c", r=2, i=PARTS)
        kparts = [kparts[:, 0], kparts[:, 1], kparts_ab[:, 0], kparts_ab[:, 1]]
        sq_q, sq_k, sq_ctx = squares[:, 0:SEQ], squares[:, SEQ:2 * SEQ], squares[:, 2 * SEQ:2 * SEQ + KV]
        norm_cols = sb("norm_cols", [P, 6])
        verdict = sb("verdict", [1, 6])
        bounded = sb("bounded", [1, 2], I32)
        uneven = sb("uneven", [P, NCHUNK])
        nan_seen = sb("nan_seen", [P, 1])
        chunk_max = sb("chunk_max", [P, NCHUNK])
        neg_max = sb("neg_max", [P, 1])
        rden_gen = sb("rden_gen", [P, 1])
        share = sb("share", [P, 32])
        nan_flag = sb("nan_flag", [32, 1], I32)
        logits = sb("logits", [P, NBLK, E])
        top = sb("top", [P, NBLK, 8])
        top_at = sb("top_at", [P, NBLK, 8], U32)
        top_f = sb("top_f", [P, NBLK, 2])
        gates = sb("gates", [P, NBLK, 2])
        gap = sb("gap", [P, NBLK])
        gap_exp = sb("gap_exp", [P, NBLK])
        expert_no = sb("expert_no", [P, NBLK, E])
        pick = logits
        combine = top
        logitsT = attnT[0:E, :]
        combineT = attnT[0:E, :]
        yT = turned
        result = xn

        scores = stack.enter_context(nc.psum_tensor("scores", [P, 2, 3, HALF], F32))
        outs = stack.enter_context(nc.psum_tensor("outs", [P, NHALF, HALF], F32))

        def bank(b):
            return scores[:, b // 3, b % 3, :] if b < 6 else outs[:, b - 6, :]

        ks_dram = nc.dram_tensor("ks_parts", (PARTS, D, SEQ), BF16).ap()
        qs_dram = nc.dram_tensor("qs_parts", (PARTS, D, SEQ), BF16).ap()
        kc_dram = nc.dram_tensor("kc_parts", (PARTS, D, KV), BF16).ap()
        qc_dram = nc.dram_tensor("qc_parts", (PARTS, D, SEQ), BF16).ap()

        s = {}
        for name in (
            "x_loaded0 x_loaded1 wself_loaded ctx_loaded0 ctx_loaded1 ctx_loaded2 ctx_loaded3 wctx_loaded wlate_loaded wffn_loaded "
            "ident_made consts_made slots_cleared outs_cleared ones_made dve_step "
            "norm_done normT_ps normT_done qkself_ps qkself_split vself_ps vself_done self_stored "
            "ctxT_ps ctxT_done ctailT_done kctx_ps kctx_first kctx_split vctx_ps vctx_done tail_done "
            "attnT_ps attnT_done proj_ps resid_done qcross_ps qcross_split cross_stored tail_ps tail_exp "
            "b_ps b_done cb_done router_ps logitsT_done logits_ps y_scaled qkself_first qcross_first gap_done gap_exp_done combine_done combineT_ps combineT_done "
            "cb_ps hid_ps hid_relu hid_used yT_done y_ps out_done out_stored "
            "sq_self norms_self sq_ctx norms_ctx sq_cross norms_cross cols_done colsT_ps bounded_made "
            "general_step general_pool kept_all pool_step fold_made spread_made kctx_stored0 kctx_stored1 kctx_stored2 kctx_stored3 turned_cleared ktail_made"
        ).split():
            s[name] = sem(name)
        L = []
        for phase in ("self", "cross"):
            L.append({n: sem(f"{phase}_{n}") for n in (
                "qk_done exp_done pv_batches turned0 turned1 folded0 folded1 "
                "kept0 kept1 rden0 rden1 kq_loaded0 kq_loaded1 v_loaded0 v_loaded1").split()})

        G = [{n: sem(f"general{ph}_{n}") for n in (
            "kq v mask round scored copied maxed exped tail turned_ps turned pv dve "
            "uniform nan_ps").split()} for ph in range(2)]
        KQ_DMAS = PARTS + PARTS
        plans = [self_plan(), cross_plan()]
        rings = [SRING, RING]
        SC = [SELF_SCALE, CROSS_SCALE]

        def layout(ph):
            groups, batches = plans[ph]
            where = {(t, hf): (g, b, q0, n, col) for g, banks in enumerate(groups)
                     for b, pieces in enumerate(banks) for t, hf, q0, n, col in pieces}
            all_groups = [(hh, g) for hh in range(2) for g in range(len(groups))]
            all_batches = []
            for hh in range(2):
                for hf, members in batches:
                    last = max(where[m][0] for m in members if m in where)
                    all_batches.append((hh, hf, members, hh * len(groups) + last))
            return groups, where, all_groups, all_batches

        def batches_through(ph, g):
            _, where, all_groups, all_batches = layout(ph)
            n = len(plans[ph][0])
            need = 0
            for i, (hh, hf, members, _) in enumerate(all_batches):
                if any(m in where and hh * n + where[m][0] <= g for m in members):
                    need = i + 1
            return need

        keys_of = (SEQ, KV)
        chunks_of = [-(-n // HALF) for n in keys_of]
        tiles_of = (NBLK, KT)

        def wrapped_fold(ph, hf):
            return 1 if ph == 0 or hf == halves_of[ph][-1] else 0

        halves_of = ((1, 0), (0, 1))

        def choose(eng, ph, fast, general):
            eng.wait_ge(s["bounded_made"], ph + 1)
            within = eng.value_load(bounded[0:1, ph:ph + 1], min_val=0, max_val=1)
            eng.cond(within, fast, general)

        def raw(c, w=HALF):
            return probs[:, c // 3, c % 3, 0:w] if c < 3 * RING else rest[:, 0:w]

        mask_wide = k_slot[1][:, 0:2 * SEQ - P]

        def batches_of(ph):
            return len(layout(ph)[3])

        def half_summed(ph, i, hh, hf):
            last = max(n for n, b in enumerate(layout(ph)[3]) if b[:2] == (hh, hf))
            return i * batches_of(ph) + batches_of(ph) + last + 1

        block = stack.enter_context(nc.Block())

        @block.sync
        def _(sp):
            x_v = x[0].rearrange("(b p) d -> p b d", p=P)
            for hf in range(NHALF):
                sp.dma_start(x_sb[:, 4 * hf:4 * hf + 4, :], x_v[:, 4 * hf:4 * hf + 4, :])\
                    .then_inc(s[f"x_loaded{hf}"], 16)
            sp.dma_start(wqvk_sb[:, :], wqvk).then_inc(s["wself_loaded"], 16)
            ctx_keys = ctx[0, 0:KT * P, :].rearrange("(p t) c -> p t c", t=KT)
            sp.dma_start(wk_sb[0:C, :], wk).then_inc(s["wctx_loaded"], 16)
            sp.dma_start(wk_sb[C:C + 1, :], bk.rearrange("(a n) -> a n", a=1)).then_inc(s["wctx_loaded"], 16)
            sp.dma_start(wv_sb[0:C, :], wv).then_inc(s["wctx_loaded"], 16)
            sp.dma_start(wv_sb[C:C + 1, :], bv.rearrange("(a n) -> a n", a=1)).then_inc(s["wctx_loaded"], 16)
            for n, (a, b) in enumerate(((0, 8), (8, 20), (20, 34), (34, KT))):
                sp.dma_start(ctx_sb[:, a:b, :], ctx_keys[:, a:b, :]).then_inc(s[f"ctx_loaded{n}"], 16)
            sp.dma_start(ctail[:, :], ctx[0, KT * P:KV, :]).then_inc(s["wctx_loaded"], 16)
            for dst, src in ((wos_sb[:, :], wo_s), (wq_sb[:, :], wq), (wox_sb[:, :], wo_x),
                             (bq_sb[:, :], bq.rearrange("(n a) -> n a", a=1)),
                             (bo_rows[:, :], bo.rearrange("(a n) -> a n", a=1).to_broadcast([P, D])),
                             (rw_sb[:, :], rw), (rb_sb[:, :], rb.rearrange("(n a) -> n a", a=1)),
                             (b1_rows[:, :], b1.rearrange("e (f p) -> (e f) p", p=P)),
                             (b2_sb[:, :], b2)):
                sp.dma_start(dst, src).then_inc(s["wlate_loaded"], 16)

            def load_head(ph, slot, head, n_keys, loaded=None, which="kq"):
                loaded = loaded or L[ph][f"kq_loaded{slot}"]
                k_dram, q_dram = ((ks_dram, qs_dram), (kc_dram, qc_dram))[ph]
                for j in range(PARTS if "k" in which else 0):
                    sp.dma_start(k_slot[slot][24 * j:24 * j + 24, 0:n_keys],
                                 k_dram[:, bass.ds(head * HD, HD), :]).then_inc(loaded, 16)
                for j in range(PARTS if "q" in which else 0):
                    sp.dma_start(q_slot[slot][24 * j:24 * j + 24, :],
                                 q_dram[j, bass.ds(head * HD, HD), :].unsqueeze(0)
                                 .to_broadcast([PARTS, HD, SEQ])).then_inc(loaded, 16)

            def load_next_heads(ph):
                with sp.Fori(0, ITERS - 1) as i:
                    for slot in range(2):
                        sp.wait_ge(L[ph]["qk_done"], (i * 2 + slot + 1) * len(plans[ph][0]))
                        load_head(ph, slot, i * 2 + slot + 2, keys_of[ph])
                sp.wait_ge(L[ph]["qk_done"], (H - 1) * len(plans[ph][0]))
                load_head(ph, 0, 0, keys_of[ph])
                sp.wait_ge(L[ph]["qk_done"], H * len(plans[ph][0]) + 2)

            def load_general(ph):
                for slot in range(2):
                    sp.wait_ge(L[ph][f"kq_loaded{slot}"], 16 * KQ_DMAS)
                with sp.Fori(0, H) as h:
                    sp.wait_ge(G[ph]["round"], h * NBLK + 1)
                    load_head(ph, 0, h, keys_of[ph], G[ph]["kq"])
                sp.wait_ge(G[ph]["round"], H * NBLK + 1)

            sp.wait_ge(s["qkself_split"], 4)
            sp.dma_start(qs_dram.rearrange("i p c -> p i c"), qparts[:, :, :]).then_inc(s["self_stored"], 16)
            sp.dma_start(ks_dram.rearrange("i p c -> p i c"), ksparts[:, :, :]).then_inc(s["self_stored"], 16)
            sp.wait_ge(s["slots_cleared"], 4)
            sp.wait_ge(s["self_stored"], 32)
            for c in range(NCHUNK - 1):
                sp.wait_ge(s["kctx_split"], c + 1)
                sp.dma_start(kc_dram[:, :, c * CHUNK * P:(c + 1) * CHUNK * P].rearrange("i p c -> p i c"),
                             kparts[c % KRING]).then_inc(s[f"kctx_stored{c % KRING}"], 16)
                if c == 0:
                    for slot in range(2):
                        load_head(0, slot, slot, SEQ)
            c, w = NCHUNK - 1, KV - (NCHUNK - 1) * CHUNK * P
            sp.wait_ge(s["kctx_split"], NCHUNK)
            sp.dma_start(kc_dram[:, :, c * CHUNK * P:KV].rearrange("i p c -> p i c"),
                         kparts[c % KRING][:, :, 0:w]).then_inc(s[f"kctx_stored{c % KRING}"], 16)
            sp.wait_ge(s["tail_done"], 1)
            sp.wait_ge(s["vctx_done"], NCHUNK)
            sp.dma_start(w1_sb, w1.rearrange("e d f -> d e f")).then_inc(s["wffn_loaded"], 16)
            sp.dma_start(w2_sb, w2.rearrange("e (f p) d -> p e f d", p=P)).then_inc(s["wffn_loaded"], 16)
            choose(sp, 0, lambda: load_next_heads(0), lambda: load_general(0))
            for n in range(KRING):
                sp.wait_ge(s[f"kctx_stored{n}"], 16 * len(range(n, NCHUNK, KRING)))
            for slot in range(2):
                load_head(1, slot, slot, KV, which="k")
            sp.wait_ge(s["qcross_split"], 2)
            sp.dma_start(qc_dram.rearrange("i p c -> p i c"), qparts[:, :, :]).then_inc(s["cross_stored"], 16)
            sp.wait_ge(s["cross_stored"], 16)
            for slot in range(2):
                load_head(1, slot, slot, KV, which="q")
            choose(sp, 1, lambda: load_next_heads(1), lambda: load_general(1))
            out_v = out[0].rearrange("(b p) d -> p b d", p=P)
            for hf in range(NHALF):
                sp.wait_ge(s["out_done"], hf + 1)
                sp.dma_start(out_v[:, 4 * hf:4 * hf + 4, :], result[:, 4 * hf:4 * hf + 4, :]).then_inc(s["out_stored"], 16)
            sp.wait_ge(s["out_stored"], 16 * NHALF)

        @block.gpsimd
        def _(pool):
            made = {}

            def after(ins, what="pool_step"):
                made[what] = made.get(what, 0) + 1
                ins.then_inc(s[what], 1)
                pool.wait_ge(s[what], made[what])

            after(pool.memset(ident[:, :], 0.0))
            after(pool.affine_select(out=ident[:, :], in_=ident[:, :], compare_op=ALU.not_equal, fill=1.0, base=0,
                               pattern=[[-1, P]], channel_multiplier=1), "ident_made")
            after(pool.memset(ctxT_region[C:C + 1, :], 1.0), "ones_made")
            after(pool.memset(ctailT[C:C + 1, :, :], 1.0), "ones_made")
            after(pool.memset(v_self[:, :, :, HD], 1.0), "ones_made")
            after(pool.memset(v_ctx[:, :, 0:KT, HD], 1.0), "ones_made")
            after(pool.memset(v_ctx[:, :, KT, :], 0.0), "ones_made")
            after(pool.memset(identb[:, :], 0.0))
            after(pool.affine_select(out=identb[:, :], in_=identb[:, :], compare_op=ALU.not_equal, fill=1.0, base=0,
                               pattern=[[-1, P]], channel_multiplier=1), "consts_made")
            after(pool.memset(causal[:, :], 0.0))
            after(pool.affine_select(out=causal[:, :], in_=causal[:, :], compare_op=ALU.is_ge, fill=MASKED, base=0,
                               pattern=[[1, P]], channel_multiplier=-1), "consts_made")
            after(pool.memset(fold[:, :, :], 0.0))
            for quad in range(4):
                after(pool.affine_select(out=fold[:, quad:4, :], in_=fold[:, quad:4, :], compare_op=ALU.not_equal,
                                         fill=1.0, base=-32 * quad, pattern=[[0, 4 - quad], [-1, 32]],
                                         channel_multiplier=1), "fold_made")
            for t, width, heads in ((head_rows, HD, P), (tail_rows, TAIL, H * TAIL)):
                after(pool.memset(t[:, :], 1.0))
                after(pool.affine_select(out=t[:, :], in_=t[:, :], compare_op=ALU.is_ge, fill=0.0, base=0,
                                         pattern=[[-width, H]], channel_multiplier=1))
                after(pool.affine_select(out=t[:, :], in_=t[:, :], compare_op=ALU.is_ge, fill=0.0, base=width - 1,
                                   pattern=[[width, H]], channel_multiplier=-1), "consts_made")
            after(pool.memset(share[:, :], 1.0 / KV), "consts_made")
            for e in range(E):
                after(pool.memset(expert_no[:, :, e], float(e)), "consts_made")

            for slot in range(2):
                after(pool.memset(k_slot[slot][:, :].bitcast(F32), 0.0), "slots_cleared")
                after(pool.memset(q_slot[slot][:, :].bitcast(F32), 0.0), "slots_cleared")
            after(pool.memset(turned[:, :, :], 0.0), "turned_cleared")

            v_all = (v_self, v_ctx)
            n_v = (NBLK, KT + 1)

            def load_v(ph):
                for slot in range(2):
                    pool.tensor_copy(v_slot[slot][:, 0:n_v[ph], :], v_all[ph][:, slot, :, :])\
                        .then_inc(L[ph][f"v_loaded{slot}"], 1)
                with pool.Fori(0, ITERS - 1) as i:
                    for slot in range(2):
                        pool.wait_ge(L[ph]["pv_batches"], half_summed(ph, i, slot, halves_of[ph][-1]))
                        pool.tensor_copy(v_slot[slot][:, 0:n_v[ph], :],
                                         v_all[ph][:, bass.ds(i * 2 + slot + 2, 1), :, :].rearrange("p a t c -> p (a t) c"))\
                            .then_inc(L[ph][f"v_loaded{slot}"], 1)
                pool.wait_ge(L[ph]["pv_batches"], (ITERS + 1) * batches_of(ph))
                for slot in range(2):
                    pool.wait_ge(L[ph][f"v_loaded{slot}"], ITERS)

            def load_v_general(ph):
                if ph == 0:
                    pool.wait_ge(L[0]["kq_loaded1"], 16 * KQ_DMAS)
                    after(pool.memset(mask_wide, 0.0), "general_pool")
                    pool.affine_select(out=mask_wide, in_=mask_wide, compare_op=ALU.is_ge, fill=MASKED, base=SEQ - P,
                                       pattern=[[-1, 2 * SEQ - P]], channel_multiplier=1).then_inc(G[0]["mask"], 1)
                    pool.wait_ge(G[0]["mask"], 1)
                with pool.Fori(0, H) as h:
                    pool.wait_ge(G[ph]["round"], h * NBLK + 1)
                    pool.tensor_copy(v_slot[0][:, 0:n_v[ph], :],
                                     v_all[ph][:, bass.ds(h, 1), :, :].rearrange("p a t c -> p (a t) c"))\
                        .then_inc(G[ph]["v"], 1)
                pool.wait_ge(G[ph]["round"], H * NBLK + 1)
                pool.wait_ge(G[ph]["v"], H)

            pool.wait_ge(s["vself_done"], 2)
            choose(pool, 0, lambda: load_v(0), lambda: load_v_general(0))
            after(pool.memset(spread[:, :, :], 0.0))
            after(pool.affine_select(out=spread[:, :, :], in_=spread[:, :, :], compare_op=ALU.not_equal, fill=1.0,
                                     base=0, pattern=[[-1, E], [0, P]], channel_multiplier=1), "spread_made")
            pool.wait_ge(s["vctx_done"], NCHUNK)
            pool.wait_ge(s["tail_done"], 1)
            choose(pool, 1, lambda: load_v(1), lambda: load_v_general(1))

        N_CONSTS = 1 + 1 + 2 + 1 + E

        @block.scalar
        def _(act):
            def evac(dst, src, done, n=1):
                act.activation(dst, src, ACT.Copy).then_inc(done, n)

            def norm_transposed(base):
                for hf in range(NHALF):
                    act.wait_ge(s["normT_ps"], base + hf + 1)
                    evac(xnT[:, hf * HALF:(hf + 1) * HALF], bank(hf), s["normT_done"])

            norm_transposed(0)
            for n in range(4):
                act.wait_ge(s["qkself_ps"], n + 1)
                here = slice(n // 2 * HALF, (n // 2 + 1) * HALF)
                act.activation((sq_q, sq_k)[n % 2][:, here], bank(2 + n), ACT.Square).then_inc(s["sq_self"], 1)
                evac((qparts, ksparts)[n % 2][:, 0, here], bank(2 + n), s["qkself_first"])
            act.wait_ge(s["ones_made"], 5)
            for hf in range(NHALF):
                act.wait_ge(s["vself_ps"], hf + 1)
                evac(v_self[:, :, 4 * hf:4 * hf + 4, 0:HD].rearrange("p h t d -> p t h d"),
                     bank(6 + hf).rearrange("p (t h d) -> p t h d", t=4, h=H), s["vself_done"])

            def ctx_transposed(c):
                w = min(CHUNK * P, KV - c * CHUNK * P)
                act.wait_ge(s["ctxT_ps"], c + 1)
                evac(ctxT_region[0:C, c * CHUNK * P:c * CHUNK * P + w], bank(c % 2)[0:C, 0:w], s["ctxT_done"])

            for c in range(min(2, NCHUNK)):
                ctx_transposed(c)
            for c in range(NCHUNK):
                w = min(CHUNK * P, KV - c * CHUNK * P)
                nt = min(CHUNK, KT - c * CHUNK)
                act.wait_ge(s["kctx_ps"], c + 1)
                if c >= KRING:
                    act.wait_ge(s[f"kctx_stored{c % KRING}"], 16 * (c // KRING))
                act.activation(sq_ctx[:, c * CHUNK * P:c * CHUNK * P + w], bank(2 + c % 2)[:, 0:w], ACT.Square)\
                    .then_inc(s["sq_ctx"], 1)
                evac(kparts[c % KRING][:, 0, 0:w], bank(2 + c % 2)[:, 0:w], s["kctx_first"])
                act.wait_ge(s["vctx_ps"], c + 1)
                evac(v_ctx[:, :, c * CHUNK:c * CHUNK + nt, 0:HD].rearrange("p h t d -> p t h d"),
                     bank(4 + c % 2)[:, 0:nt * D].rearrange("p (t h d) -> p t h d", t=nt, h=H), s["vctx_done"])
                if c + 2 < NCHUNK:
                    ctx_transposed(c + 2)

            def exponentials(ph):
                _, _, all_groups, all_batches = layout(ph)
                groups = plans[ph][0]
                n, ring, nb = len(all_groups), rings[ph], len(all_batches)
                if ph == 1:
                    for hf in range(NHALF):
                        act.wait_ge(s["tail_ps"], hf + 1)
                        act.activation(ptail[:, hf * HALF:(hf + 1) * HALF], bank(4 + hf)[0:H * TAIL, :], ACT.Exp,
                                       scale=CROSS_SCALE).then_inc(s["tail_exp"], 1)
                with act.Fori(0, ITERS) as i:
                    for g, (hh, gg) in enumerate(all_groups):
                        nbanks = len(groups[gg])
                        act.wait_ge(L[ph]["qk_done"], i * n + g + 1)
                        if g >= ring:
                            need = nb + batches_through(ph, g - ring)
                        else:
                            need = batches_through(ph, n + g - ring)
                        act.wait_ge(L[ph]["pv_batches"], i * nb + need)
                        act.activation(probs[:, g % ring, 0:nbanks, :], scores[:, g % 2, 0:nbanks, :], ACT.Exp,
                                       scale=SC[ph]).then_inc(L[ph]["exp_done"], 1)

            def general_exponentials(ph):
                nc_, keys = chunks_of[ph], keys_of[ph]
                with act.Fori(0, H) as h:
                    with act.Fori(0, NBLK) as b:
                        n = h * NBLK + b
                        act.wait_ge(G[ph]["maxed"], n + 1)
                        for c in range(nc_):
                            w = min(HALF, keys - c * HALF)
                            act.activation(raw(c, w), raw(c, w), ACT.Exp, bias=neg_max[:, 0:1])\
                                .then_inc(G[ph]["exped"], 1)
                        for c in range(nc_):
                            act.wait_ge(G[ph]["turned_ps"], n * nc_ + c + 1)
                            if c >= 2:
                                act.wait_ge(G[ph]["pv"], n * nc_ + c - 1)
                            w = min(HALF, (tiles_of[ph] * P - c * HALF))
                            ins = act.activation(turned[:, c % 2, 0:w], bank(2 + c % 2)[:, 0:w], ACT.Copy)
                            if ph == 1 and c == nc_ - 1:
                                ins = act.activation(turned[0:H * TAIL, c % 2, w:w + P],
                                                     bank(2 + c % 2)[0:H * TAIL, w:w + P], ACT.Copy)
                            ins.then_inc(G[ph]["turned"], 1)

            for n in range(KRING):
                act.wait_ge(s[f"kctx_stored{n}"], 16 * len(range(n, NCHUNK, KRING)))
            choose(act, 0, lambda: exponentials(0), lambda: general_exponentials(0))

            def heads_transposed(base):
                for hf in range(NHALF):
                    act.wait_ge(s["attnT_ps"], base + hf + 1)
                    evac(attnT[:, hf * HALF:(hf + 1) * HALF], bank(hf), s["attnT_done"])

            heads_transposed(0)
            norm_transposed(2)
            for hf in range(NHALF):
                act.wait_ge(s["qcross_ps"], hf + 1)
                act.activation(sq_q[:, hf * HALF:(hf + 1) * HALF], bank(4 + hf), ACT.Square,
                               bias=bq_sb[:, 0:1]).then_inc(s["sq_cross"], 1)
                act.wait_ge(s["self_stored"], 32)
                act.activation(qparts[:, 0, hf * HALF:(hf + 1) * HALF], bank(4 + hf), ACT.Identity,
                               bias=bq_sb[:, 0:1]).then_inc(s["qcross_first"], 1)
            choose(act, 1, lambda: exponentials(1), lambda: general_exponentials(1))
            heads_transposed(2)
            act.wait_ge(s["b_ps"], 1)
            act.activation(b1_sb[:, :], bank(5)[:, 0:E * NF], ACT.Copy)
            evac(b2T_sb[:, :], bank(5)[:, E * NF:E * NF + E], s["b_done"])
            norm_transposed(4)
            for hf in range(NHALF):
                act.wait_ge(s["router_ps"], hf + 1)
                act.activation(logitsT[:, hf * HALF:(hf + 1) * HALF], bank(6 + hf)[0:E, :], ACT.Identity,
                               bias=rb_sb[:, 0:1]).then_inc(s["logitsT_done"], 1)
            act.wait_ge(s["b_done"], 1)
            for n in range(NHALF * E * NF):
                e, f = n // NF % E, n % NF
                act.wait_ge(s["hid_ps"], n + 1)
                if n >= RING:
                    act.wait_ge(s["hid_used"], n - RING + 1)
                act.activation(hidden[:, n % RING, :], bank(n % 4), ACT.Relu,
                               bias=b1_sb[:, e * NF + f:e * NF + f + 1]).then_inc(s["hid_relu"], 1)
                if n == 3:
                    act.wait_ge(s["gap_done"], 1)
                    act.activation(gap_exp[:, :], gap[:, :], ACT.Exp).then_inc(s["gap_exp_done"], 1)
                for m in ((0, 1) if n == 7 else (n // NF,) if n > 8 and n % NF == LAG else ()):
                    act.wait_ge(s["cb_ps"], m + 1)
                    if m >= 2:
                        act.wait_ge(s["y_scaled"], m - 1)
                    evac(gate_rows[:, m % 2, :], bank(4 + m % 2), s["cb_done"])
                if n == 5:
                    for hf in range(NHALF):
                        act.wait_ge(s["combineT_ps"], hf + 1)
                        evac(combineT[:, hf * HALF:(hf + 1) * HALF], bank(4 + hf)[0:E, :], s["combineT_done"])

        @block.vector
        def _(dve):
            made = {}

            def step(ins, what="dve_step"):
                made[what] = made.get(what, 0) + 1
                ins.then_inc(s[what], 1)
                dve.wait_ge(s[what], made[what])

            def stats_of(hf):
                for b in range(4 * hf, 4 * hf + 4):
                    ins = dve.bn_stats(stats[:, b, :], x_sb[:, b, :])
                step(ins)
                for b in range(4 * hf, 4 * hf + 4):
                    ins = dve.bn_aggr(mv[:, b, :], stats[:, b, :])
                step(ins)

            def normalise_rows():
                step(dve.tensor_scalar(var[:, :], mv[:, :, 1], EPS, None, ALU.add))
                step(dve.tensor_scalar(rstd[:, :].bitcast(I32), var[:, :].bitcast(I32), 1, None,
                                       ALU.logical_shift_right))
                step(dve.tensor_scalar(rstd[:, :].bitcast(I32), rstd[:, :].bitcast(I32), -1.0, float(0x5F3759DF),
                                       ALU.mult, ALU.add))
                for _ in range(4):
                    step(dve.scalar_tensor_tensor(newton[:, :], rstd[:, :], -0.5, rstd[:, :], ALU.mult, ALU.mult))
                    step(dve.tensor_tensor(newton[:, :], newton[:, :], var[:, :], ALU.mult))
                    step(dve.scalar_tensor_tensor(rstd[:, :], newton[:, :], 1.5, rstd[:, :], ALU.add, ALU.mult))
                for b in range(NBLK):
                    ins = dve.tensor_scalar(xn[:, b, :], x_sb[:, b, :], mv[:, b, 0:1], rstd[:, b:b + 1],
                                            ALU.subtract, ALU.mult)
                    if b % 4 == 3:
                        step(ins, "norm_done")

            def split(src, parts, done, bias=None, first=True):
                w = src.shape[-1]
                r = rest[:, 0:w]
                if bias is None:
                    if first:
                        step(dve.tensor_copy(parts[0], src))
                    step(dve.tensor_tensor(r, src, parts[0], ALU.subtract))
                else:
                    step(dve.scalar_tensor_tensor(r, src, bias, parts[0], ALU.add, ALU.subtract))
                step(dve.tensor_copy(parts[1], r))
                step(dve.tensor_tensor(parts[2], r, parts[1], ALU.subtract), done)

            for hf in range(NHALF):
                dve.wait_ge(s[f"x_loaded{hf}"], 16)
                stats_of(hf)
            normalise_rows()
            for n in range(4):
                dst = (qparts, ksparts)[n % 2]
                hf = n // 2
                dve.wait_ge(s["qkself_first"], n + 1)
                split(bank(2 + n), [dst[:, i, hf * HALF:(hf + 1) * HALF] for i in range(PARTS)],
                      "qkself_split", first=False)
            def norm_columns(src, n, at):
                dve.tensor_reduce(norm_cols[:, at:at + 1], src[:, 0:n], AX.X, ALU.max)
                step(dve.tensor_reduce(norm_cols[:, at + 1:at + 2], src[:, 0:n], AX.X, ALU.add), "cols_done")

            def judge(ph):
                limit = (BOUND / (SELF_SCALE, CROSS_SCALE)[ph]) ** 2 / SLACK
                dve.wait_ge(s["colsT_ps"], ph + 1)
                rows = bank(7)[0:1, :].rearrange("p (c n) -> p c n", c=4)
                dve.tensor_reduce(verdict[:, 0:2], rows[:, 0:2, :], AX.X, ALU.max)
                step(dve.tensor_reduce(verdict[:, 2:4], rows[:, 2:4, :], AX.X, ALU.add))
                dve.tensor_scalar(verdict[:, 4:5], verdict[:, 0:1], verdict[:, 1:2], limit, ALU.mult, ALU.is_le)
                step(dve.tensor_scalar(verdict[:, 5:6], verdict[:, 2:3], verdict[:, 3:4], FINITE, ALU.add, ALU.is_le))
                step(dve.tensor_tensor(bounded[:, ph:ph + 1], verdict[:, 4:5], verdict[:, 5:6], ALU.mult), "bounded_made")

            for c in range(NCHUNK):
                w = min(CHUNK * P, KV - c * CHUNK * P)
                if c == 2:
                    dve.wait_ge(s["norms_self"], 1)
                    for n in range(2):
                        norm_columns(bank(6)[:, n * NBLK * H:(n + 1) * NBLK * H], NBLK * H, 2 * n)
                if c == 3:
                    judge(0)
                if c == NCHUNK - 1:
                    dve.wait_ge(s["ones_made"], 2)
                    dve.wait_ge(s["ctxT_done"], NCHUNK)
                    dve.tensor_copy(ctailT[0:C, :, :], ctxT_region[0:C, KT * P:KV].unsqueeze(1)
                                    .to_broadcast([C, H, TAIL])).then_inc(s["ctailT_done"], 1)
                    w0 = KT * P - c * CHUNK * P
                    dve.wait_ge(s["kctx_first"], c + 1)
                    split(bank(2 + c % 2)[:, 0:w], [kparts[c % KRING][:, i, 0:w] for i in range(PARTS)],
                          "dve_step", first=False)
                    step(dve.tensor_copy(ktail[:, :, :], kparts[c % KRING][:, :, w0:w]), "kctx_split")
                else:
                    dve.wait_ge(s["kctx_first"], c + 1)
                    split(bank(2 + c % 2)[:, 0:w], [kparts[c % KRING][:, i, 0:w] for i in range(PARTS)],
                          "kctx_split", first=False)
            dve.wait_ge(s["consts_made"], N_CONSTS)
            dve.wait_ge(s["vctx_ps"], NCHUNK)
            dve.wait_ge(s["vctx_done"], NCHUNK)
            dve.tensor_tensor(v_ctx[0:H * TAIL, :, KT, 0:HD],
                              bank(4 + (NCHUNK - 1) % 2)[0:H * TAIL, 2 * D:3 * D].rearrange("p (h d) -> p h d", h=H),
                              tail_rows[:, :].unsqueeze(2).to_broadcast([H * TAIL, H, HD]), ALU.mult)
            dve.tensor_copy(v_ctx[0:H * TAIL, :, KT, HD], tail_rows[:, :]).then_inc(s["tail_done"], 1)
            dve.wait_ge(s["norms_ctx"], 1)
            norm_columns(bank(6), HALF, 0)
            norm_columns(bank(7), (KT + 1) * H - HALF, 2)
            dve.memset(outs[:, :, :], 0.0).then_inc(s["outs_cleared"], 1)
            step(dve.tensor_tensor(norm_cols[:, 2:3], norm_cols[:, 2:3], norm_cols[:, 0:1], ALU.max))
            step(dve.tensor_tensor(norm_cols[:, 3:4], norm_cols[:, 3:4], norm_cols[:, 1:2], ALU.add))
            dve.wait_ge(s["kctx_split"], NCHUNK)
            for i in range(PARTS):
                ins = dve.tensor_tensor(ktail_heads[:, i, :, :], ktail[:, i:i + 1, :].to_broadcast([P, H, TAIL]),
                                        head_rows[:, :].unsqueeze(2).to_broadcast([P, H, TAIL]), ALU.mult)
            ins.then_inc(s["ktail_made"], 1)

            def normalise(ph):
                with dve.Fori(0, ITERS) as i:
                    for hh in range(2):
                        for hf in halves_of[ph]:
                            dve.wait_ge(L[ph]["pv_batches"], half_summed(ph, i, hh, hf))
                            dve.transpose(turned[:, hf, :], outs[:, hf, :]).then_inc(L[ph][f"turned{hf}"], 1)
                            dve.wait_ge(L[ph][f"folded{hf}"], i * 2 + hh + 1 + wrapped_fold(ph, hf))
                            got = outs[0:32, hf, 0:HALF // 32 * VC].rearrange("p (c v) -> p c v", v=VC)
                            dve.reciprocal(rden[:, hf, :], got[:, :, HD]).then_inc(L[ph][f"rden{hf}"], 1)
                            dve.wait_ge(L[ph][f"rden{hf}"], i * 2 + hh + 1)
                            nb = HALF // 32
                            dst = heads_out[:, hf * nb:(hf + 1) * nb, bass.ds(i * 2 + hh, 1), :]\
                                .rearrange("p c a d -> p c (a d)")
                            dve.tensor_tensor(dst, got[:, :, 0:HD],
                                              rden[:, hf, :].unsqueeze(2).to_broadcast([32, nb, HD]),
                                              ALU.mult).then_inc(L[ph][f"kept{hf}"], 1)

            def general_rows(ph):
                nc_, keys = chunks_of[ph], keys_of[ph]
                scale = (SELF_SCALE, CROSS_SCALE)[ph]
                steps_in_round = [0]

                def then(ins, n, per_round):
                    steps_in_round[0] += 1
                    ins.then_inc(G[ph]["dve"], 1)
                    dve.wait_ge(G[ph]["dve"], n * per_round + steps_in_round[0])

                per_round = {0: 2, 1: 4}[ph]
                if ph == 1:
                    step(dve.memset(nan_seen[:, :], 0.0), "general_step")
                with dve.Fori(0, H) as h:
                    with dve.Fori(0, NBLK) as b:
                        n = h * NBLK + b
                        steps_in_round[0] = 0
                        if ph == 0:
                            dve.wait_ge(G[0]["mask"], 1)
                        for c in range(nc_):
                            w = min(HALF, keys - c * HALF)
                            dve.wait_ge(G[ph]["scored"], n * nc_ + c + 1)
                            src = bank(c % 2)[:, 0:w]
                            if ph == 0:
                                at = b * -P + ((NBLK - 1) * P + c * HALF)
                                ins = dve.scalar_tensor_tensor(raw(c, w), src, scale, mask_wide[:, bass.ds(at, w)],
                                                               ALU.mult, ALU.add)
                            else:
                                ins = dve.tensor_scalar(raw(c, w), src, scale, None, ALU.mult)
                            ins.then_inc(G[ph]["copied"], 1)
                        dve.wait_ge(G[ph]["copied"], (n + 1) * nc_)
                        if ph == 1:
                            for c in range(nc_):
                                w = min(HALF, keys - c * HALF)
                                ins = dve.tensor_tensor(turned[:, 0, 0:w], raw(c, w), raw(c, w), ALU.not_equal)
                                ins.then_inc(G[ph]["uniform"], 1)
                                dve.wait_ge(G[ph]["uniform"], n * 2 * nc_ + 2 * c + 1)
                                ins = dve.tensor_reduce(uneven[:, c:c + 1], turned[:, 0, 0:w], AX.X, ALU.max)
                                ins.then_inc(G[ph]["uniform"], 1)
                                dve.wait_ge(G[ph]["uniform"], n * 2 * nc_ + 2 * c + 2)
                                ins = dve.tensor_scalar(raw(c, w), raw(c, w), CLAMP, -CLAMP, ALU.min, ALU.max)
                            then(ins, n, per_round)
                            dve.tensor_reduce(turned[:, 1, 0:1], uneven[:, 0:nc_], AX.X, ALU.max)\
                                .then_inc(G[ph]["nan_ps"], 1)
                            dve.wait_ge(G[ph]["nan_ps"], n * 2 + 1)
                            dve.tensor_tensor(nan_seen[:, :], nan_seen[:, :], turned[:, 1, 0:1], ALU.max)\
                                .then_inc(G[ph]["nan_ps"], 1)
                            dve.wait_ge(G[ph]["nan_ps"], n * 2 + 2)
                        for c in range(nc_):
                            w = min(HALF, keys - c * HALF)
                            ins = dve.tensor_reduce(chunk_max[:, c:c + 1], raw(c, w), AX.X, ALU.max)
                        then(ins, n, per_round)
                        then(dve.tensor_reduce(neg_max[:, :], chunk_max[:, 0:nc_], AX.X, ALU.max), n, per_round)
                        dve.tensor_scalar(neg_max[:, :], neg_max[:, :], -1.0, None, ALU.mult).then_inc(G[ph]["maxed"], 1)
                        if ph == 1:
                            dve.wait_ge(G[ph]["exped"], (n + 1) * nc_)
                            at = KV - TAIL - (nc_ - 1) * HALF
                            dve.tensor_copy(top[:, :, :].rearrange("p b e -> p (b e)").rearrange("p (h t) -> p h t", h=H),
                                            raw(nc_ - 1)[:, at:at + TAIL].unsqueeze(1).to_broadcast([P, H, TAIL]))\
                                .then_inc(G[ph]["tail"], 1)
                        dve.wait_ge(G[ph]["pv"], (n + 1) * nc_)
                        ins = dve.reciprocal(rden_gen[:, :], outs[:, 0, HD:HD + 1])
                        if ph == 1:
                            then(ins, n, per_round)
                        else:
                            ins.then_inc(G[ph]["uniform"], 1)
                            dve.wait_ge(G[ph]["uniform"], n + 1)
                        for quad in range(4):
                            dst = heads_out[:, bass.ds(b * 4 + quad, 1), bass.ds(h, 1), :].rearrange("p b a d -> p (b a d)")
                            ins = dve.tensor_scalar(dst, outs[32 * quad:32 * quad + 32, 0, 0:HD],
                                                    rden_gen[32 * quad:32 * quad + 32, :], None, ALU.mult)
                        ins.then_inc(G[ph]["round"], 1)
                dve.wait_ge(G[ph]["round"], H * NBLK + 1)
                if ph == 1:
                    step(dve.tensor_scalar(nan_seen[:, :], nan_seen[:, :], 0.0, None, ALU.is_gt), "general_step")
                    dve.sem_inc(G[ph]["mask"], 1)
                    dve.wait_ge(G[ph]["tail"], H * NBLK + 1)
                    mean = turned[0:32, 0, 0:D]
                    step(dve.tensor_copy(mean, outs[0:32, 1, 0:D]), "general_step")
                    step(dve.tensor_scalar(nan_flag[:, :], outs[0:32, 1, D:D + 1], 0.0, None, ALU.is_gt), "general_step")
                    for b in range(SEQ // 32):
                        ins = dve.copy_predicated(heads_out[:, b, :, :].rearrange("p h d -> p (h d)"),
                                                  nan_flag[:, :].to_broadcast([32, D]), mean)
                    step(ins, "general_step")

            def both_kept(ph):
                step(dve.tensor_copy(verdict[:, 0:1], verdict[:, 1:2]), "kept_all")

            def fast_rows(ph):
                normalise(ph)
                for hf in range(NHALF):
                    dve.wait_ge(L[ph][f"kept{hf}"], H + 1)

            choose(dve, 0, lambda: fast_rows(0), lambda: general_rows(0))
            both_kept(0)

            def residual(base):
                for hf in range(NHALF):
                    dve.wait_ge(s["proj_ps"], base + hf + 1)
                    step(dve.tensor_tensor(x_sb[:, 4 * hf:4 * hf + 4, :],
                                           bank(2 + hf).rearrange("p (b d) -> p b d", d=D),
                                           x_sb[:, 4 * hf:4 * hf + 4, :], ALU.add))
                    stats_of(hf)

            residual(0)
            normalise_rows()
            dve.wait_ge(s["wlate_loaded"], 16 * 9)
            for hf in range(NHALF):
                dve.wait_ge(s["qcross_first"], hf + 1)
                split(bank(4 + hf), [qparts[:, i, hf * HALF:(hf + 1) * HALF] for i in range(PARTS)],
                      "qcross_split", bias=bq_sb[:, 0:1], first=False)
                if hf == 0:
                    dve.wait_ge(s["norms_cross"], 1)
                    norm_columns(bank(6), NBLK * H, 0)
            judge(1)
            step(dve.tensor_tensor(x_sb[:, :, :], x_sb[:, :, :], bo_rows[:, :].unsqueeze(1).to_broadcast([P, NBLK, D]),
                                   ALU.add))
            choose(dve, 1, lambda: fast_rows(1), lambda: general_rows(1))
            both_kept(1)
            residual(2)
            normalise_rows()
            dve.wait_ge(s["logits_ps"], 1)
            step(dve.tensor_copy(logits[:, :, :], bank(5)[:, 0:NBLK * E].rearrange("p (b e) -> p b e", e=E)))
            for b in range(NBLK):
                ins = dve.max(top[:, b, :], logits[:, b, :])
            step(ins)
            for b in range(NBLK):
                ins = dve.max_index(top_at[:, b, :], top[:, b, :], logits[:, b, :])
            step(ins)
            dve.tensor_copy(top_f[:, :, :], top_at[:, :, 0:2])
            dve.tensor_tensor(gap[:, :], top[:, :, 1], top[:, :, 0], ALU.subtract).then_inc(s["gap_done"], 1)
            dve.wait_ge(s["gap_exp_done"], 1)
            step(dve.tensor_scalar(gates[:, :, 1], gap_exp[:, :], 1.0, None, ALU.add))
            step(dve.reciprocal(gates[:, :, 0], gates[:, :, 1]))
            step(dve.tensor_tensor(gates[:, :, 1], gap_exp[:, :], gates[:, :, 0], ALU.mult))
            for k, dst in ((0, combine), (1, pick)):
                step(dve.tensor_tensor(dst[:, :, :], expert_no[:, :, :],
                                       top_f[:, :, k:k + 1].to_broadcast([P, NBLK, E]), ALU.is_equal))
                step(dve.tensor_tensor(dst[:, :, :], dst[:, :, :],
                                       gates[:, :, k:k + 1].to_broadcast([P, NBLK, E]), ALU.mult))
            dve.tensor_tensor(combine[:, :, :], combine[:, :, :], pick[:, :, :], ALU.add).then_inc(s["combine_done"], 1)
            for m in range(NHALF * E):
                hf, e = m // E, m % E
                dve.wait_ge(s["cb_done"], m + 1)
                dve.wait_ge(s["hid_used"], (m + 1) * NF)
                dst = yT[:, hf, :] if e == 0 else rest[:, :]
                step(dve.scalar_tensor_tensor(dst, bank(6 + m % 2), b2T_sb[:, e:e + 1], gate_rows[:, m % 2, :],
                                              ALU.add, ALU.mult), "y_scaled")
                if e > 0:
                    step(dve.tensor_tensor(yT[:, hf, :], yT[:, hf, :], rest[:, :], ALU.add),
                         "yT_done" if e == E - 1 else "dve_step")
            for hf in range(NHALF):
                dve.wait_ge(s["y_ps"], hf + 1)
                dve.tensor_tensor(result[:, 4 * hf:4 * hf + 4, :], bank(hf).rearrange("p (b d) -> p b d", d=D),
                                  x_sb[:, 4 * hf:4 * hf + 4, :], ALU.add).then_inc(s["out_done"], 1)

        @block.tensor
        def _(pe):
            def transpose_norm(base):
                for b in range(NBLK):
                    if b % 4 == 0:
                        pe.wait_ge(s["norm_done"], base + b // 4 + 1)
                    mm = pe.transpose(bank(b // 4)[:, b % 4 * P:(b % 4 + 1) * P], xn[:, b, :], ident[:, :])
                    if b % 4 == 3:
                        mm.then_inc(s["normT_ps"], 1)

            pe.wait_ge(s["ident_made"], 1)
            transpose_norm(0)
            pe.wait_ge(s["wself_loaded"], 16)
            for hf in range(NHALF):
                pe.wait_ge(s["normT_done"], hf + 1)
                for n, col in enumerate((0, 2 * D)):
                    pe.matmul(bank(2 + 2 * hf + n), wqvk_sb[:, col:col + D], xnT[:, hf * HALF:(hf + 1) * HALF],
                              start=True, stop=True).then_inc(s["qkself_ps"], 1)
            for b in range(NBLK):
                mm = pe.matmul(bank(6 + b // 4)[:, b % 4 * D:(b % 4 + 1) * D], xnT[:, b * P:(b + 1) * P],
                               wqvk_sb[:, D:2 * D], start=True, stop=True)
                if b % 4 == 3:
                    mm.then_inc(s["vself_ps"], 1)

            def norms(src, tile, dst, tile_col):
                return pe.matmul(dst[:, tile_col:tile_col + H], src[:, tile:tile + P], head_rows[:, :], start=True, stop=True)

            def turn_columns(ph):
                for n, col in enumerate((0, 2, 1, 3)):
                    mm = pe.transpose(bank(7)[0:1, n * P:(n + 1) * P], norm_cols[:, col:col + 1], ident[:, :])
                mm.then_inc(s["colsT_ps"], 1)

            def transpose_ctx(c):
                if c >= 2:
                    pe.wait_ge(s["ctxT_done"], c - 1)
                for t in range(c * CHUNK, min((c + 1) * CHUNK, KT)):
                    for n, at in enumerate((0, 8, 20, 34)):
                        if t == at:
                            pe.wait_ge(s[f"ctx_loaded{n}"], 16)
                    mm = pe.transpose(bank(c % 2)[0:C, t % CHUNK * P:(t % CHUNK + 1) * P], ctx_sb[:, t, :], ident[:, :])
                if c == NCHUNK - 1:
                    at = KT * P - c * CHUNK * P
                    mm = pe.transpose(bank(c % 2)[0:C, at:at + TAIL], ctail[:, :], ident[0:TAIL, 0:TAIL])
                mm.then_inc(s["ctxT_ps"], 1)

            def project_ctx(c):
                w = min(CHUNK * P, KV - c * CHUNK * P)
                pe.wait_ge(s["ctxT_done"], c + 1)
                if c < 2:
                    pe.wait_ge(s["qkself_split"], 3 + c)
                else:
                    pe.wait_ge(s["kctx_split"], c - 1)
                    pe.wait_ge(s["vctx_done"], c - 1)
                pe.matmul(bank(2 + c % 2)[:, 0:w], wk_sb[:, :], ctxT[:, c * CHUNK * P:c * CHUNK * P + w],
                          start=True, stop=True).then_inc(s["kctx_ps"], 1)
                for t in range(c * CHUNK, min((c + 1) * CHUNK, KT)):
                    mm = pe.matmul(bank(4 + c % 2)[:, t % CHUNK * D:(t % CHUNK + 1) * D], ctxT[:, t * P:(t + 1) * P],
                                   wv_sb[:, :], start=True, stop=True)
                if c == NCHUNK - 1:
                    pe.wait_ge(s["ctailT_done"], 1)
                    mm = pe.matmul(bank(4 + c % 2)[0:H * TAIL, 2 * D:3 * D], ctailT[:, :, :].rearrange("c h t -> c (h t)"),
                                   wv_sb[:, :], start=True, stop=True)
                mm.then_inc(s["vctx_ps"], 1)

            pe.wait_ge(s["normT_done"], 2)
            pe.wait_ge(s["wctx_loaded"], 16 * 5)
            for c in range(min(2, NCHUNK)):
                transpose_ctx(c)
            pe.wait_ge(s["ones_made"], 2)
            for c in range(NCHUNK):
                project_ctx(c)
                if c + 2 < NCHUNK:
                    transpose_ctx(c + 2)
                if c == 1:
                    pe.wait_ge(s["consts_made"], N_CONSTS)
                    pe.wait_ge(s["sq_self"], 4)
                    pe.wait_ge(s["vself_done"], 2)
                    for n, src in enumerate((sq_q, sq_k)):
                        for b in range(NBLK):
                            mm = norms(src, b * P, bank(6), (n * NBLK + b) * H)
                    mm.then_inc(s["norms_self"], 1)
                if c == 3:
                    pe.wait_ge(s["cols_done"], 2)
                    turn_columns(0)
            pe.wait_ge(s["sq_ctx"], NCHUNK)
            pe.wait_ge(s["bounded_made"], 1)
            for t in range(KT + 1):
                mm = norms(sq_ctx, t * P if t < KT else KV - P, bank(6 + t // 32), t % 32 * H)
            mm.then_inc(s["norms_ctx"], 1)

            def attention(ph):
                groups, where, all_groups, all_batches = layout(ph)
                n_groups, nb = len(all_groups), len(all_batches)
                n_tiles = {0: NBLK, 1: KT}[ph]

                def score_group(g, loaded, first_use):
                    hh, gg = all_groups[g]
                    if gg == 0:
                        pe.wait_ge(L[ph][f"kq_loaded{hh}"], loaded)
                    for b, pieces in enumerate(groups[gg]):
                        dst = scores[:, g % 2, b, :]
                        for t, hf, q0, n, col in pieces:
                            diagonal = ph == 0 and hf * HALF + q0 == t * P
                            mm = pe.matmul(dst[:, col:col + n], k_slot[hh][:, t * P:(t + 1) * P],
                                           q_slot[hh][:, hf * HALF + q0:hf * HALF + q0 + n],
                                           start=True, stop=True)
                            if diagonal:
                                mm = pe.matmul(dst[:, col:col + P], identb[:, :], causal[:, :],
                                               start=False, stop=True, skip_group_check=True)
                    mm.then_inc(L[ph]["qk_done"], 1)

                def output_batch(i, b):
                    hh, hf, members, last = all_batches[b]
                    if b == 0 or all_batches[b - 1][1] != hf:
                        pe.wait_ge(L[ph][f"kept{hf}"], i * 2 + hh + 1)
                        if hf == halves_of[ph][0]:
                            pe.wait_ge(L[ph][f"v_loaded{hh}"], i + 1)
                    for t, _ in members:
                        quad = 32 * (t % 4)
                        if t == n_tiles:
                            mm = pe.matmul(outs[quad:quad + VC, hf, :], v_slot[hh][0:H * TAIL, t, :],
                                           ptail[:, hf * HALF:(hf + 1) * HALF], start=False, stop=True)
                            continue
                        g, bk_, q0, n, col = where[(t, hf)]
                        g += hh * len(groups)
                        final = t + 4 > (n_tiles if ph == 1 else (3 if hf == 0 else NBLK - 1))
                        mm = pe.matmul(outs[quad:quad + VC, hf, q0:q0 + n], v_slot[hh][:, t, :],
                                       probs[:, g % rings[ph], bk_, col:col + n],
                                       start=(t < 4), stop=final)
                    mm.then_inc(L[ph]["pv_batches"], 1)

                def fold_half(i, hh, hf):
                    pe.wait_ge(L[ph][f"turned{hf}"], i * 2 + hh + 2)
                    cuts = [(n, 4 * n, 4 * n + 4) for n in range(4)] if (ph, hf) == (0, 0) else [(3, 0, 16)]
                    view = turned[:, hf, :].rearrange("p (c v) -> p c v", v=32)
                    for n, a, b in cuts:
                        mm = pe.matmul(outs[0:32, hf, a * VC:b * VC], fold[:, n, :], view[:, a:b, 0:VC],
                                       start=True, stop=True)
                    mm.then_inc(L[ph][f"folded{hf}"], 1)

                LOAD = 16 * KQ_DMAS
                pe.sem_inc(L[ph]["pv_batches"], nb)
                for hf in range(NHALF):
                    pe.sem_inc(L[ph][f"kept{hf}"], 1)
                    pe.sem_inc(L[ph][f"turned{hf}"], 1)
                score_group(0, LOAD, True)
                if ph == 1:
                    pe.wait_ge(s["tail_exp"], 2)
                score_group(1, LOAD, True)
                def run_batches(i, now):
                    while due and due[0][0] <= now:
                        output_batch(i, due.pop(0)[1])

                due = [(last, b) for b, (hh, hf, members, last) in enumerate(all_batches)]
                folds = []
                for hh in range(2):
                    for n, hf in enumerate(halves_of[ph]):
                        end = max(k for k, b in enumerate(all_batches) if b[:2] == (hh, hf))
                        if ph == 0 and n == 1 and hh == 0:
                            due[end] = (due[end][0] + 1, end)
                        folds.append(((all_batches[end][3] + (1 + n if ph == 0 else 2)), hh, hf))
                wrapped = [(at - n_groups, hh, hf) for at, hh, hf in folds if at >= n_groups]
                folds = [f for f in folds if f[0] < n_groups]
                with pe.Fori(0, ITERS) as i:
                    for g in range(n_groups):
                        nxt = g + 2
                        pe.wait_ge(L[ph]["exp_done"], i * n_groups + g + 1)
                        if nxt < n_groups:
                            score_group(nxt, i * LOAD + LOAD, False)
                        else:
                            score_group(nxt - n_groups, i * LOAD + 2 * LOAD, False)
                        for at, hh, hf in wrapped:
                            if at == g and ph == 0 and hf == halves_of[ph][0]:
                                fold_half(i, hh - 2, hf)
                        run_batches(i, g)
                        for at, hh, hf in wrapped:
                            if at == g and not (ph == 0 and hf == halves_of[ph][0]):
                                fold_half(i, hh - 2, hf)
                        for at, hh, hf in folds:
                            if at == g:
                                fold_half(i, hh, hf)
                assert not due
                for at, hh, hf in wrapped:
                    fold_half(ITERS - 1, hh, hf)

            def general(ph):
                nc_, keys, n_tiles = chunks_of[ph], keys_of[ph], tiles_of[ph]
                pe.sem_inc(G[ph]["round"], 1)
                with pe.Fori(0, H) as h:
                    with pe.Fori(0, NBLK) as b:
                        n = h * NBLK + b
                        pe.wait_ge(G[ph]["kq"], (h + 1) * 16 * KQ_DMAS)
                        pe.wait_ge(G[ph]["v"], h + 1)
                        pe.wait_ge(G[ph]["round"], n + 1)
                        for c in range(nc_):
                            w = min(HALF, keys - c * HALF)
                            if c >= 2:
                                pe.wait_ge(G[ph]["copied"], n * nc_ + c - 1)
                            pe.matmul(bank(c % 2)[:, 0:w], q_slot[0][:, bass.ds(b * P, P)],
                                      k_slot[0][:, c * HALF:c * HALF + w], start=True, stop=True)\
                                .then_inc(G[ph]["scored"], 1)

                        def turn(c):
                            if ph == 1 and c == nc_ - 1:
                                pe.wait_ge(G[ph]["tail"], n + 1)
                            pe.wait_ge(G[ph]["exped"], n * nc_ + c + 1)
                            if c >= 2:
                                pe.wait_ge(G[ph]["turned"], n * nc_ + c - 1)
                            for t in range(4 * c, min(4 * c + 4, n_tiles)):
                                mm = pe.transpose(bank(2 + c % 2)[:, t % 4 * P:(t % 4 + 1) * P],
                                                  raw(c)[:, t % 4 * P:(t % 4 + 1) * P], ident[:, :])
                            if ph == 1 and c == nc_ - 1:
                                at = n_tiles % 4 * P
                                mm = pe.transpose(bank(2 + c % 2)[0:H * TAIL, at:at + P],
                                                  top[:, :, :].rearrange("p b e -> p (b e)"), ident[:, :])
                            mm.then_inc(G[ph]["turned_ps"], 1)

                        turn(0)
                        turn(1)
                        for c in range(nc_):
                            pe.wait_ge(G[ph]["turned"], n * nc_ + c + 1)
                            for t in range(4 * c, min(4 * c + 4, n_tiles)):
                                last = ph == 0 and t == n_tiles - 1
                                mm = pe.matmul(outs[:, 0, 0:VC], turned[:, c % 2, t % 4 * P:(t % 4 + 1) * P],
                                               v_slot[0][:, t, :], start=(t == 0), stop=last)
                            if ph == 1 and c == nc_ - 1:
                                at = n_tiles % 4 * P
                                mm = pe.matmul(outs[:, 0, 0:VC], turned[0:H * TAIL, c % 2, at:at + P],
                                               v_slot[0][0:H * TAIL, n_tiles, :], start=False, stop=True)
                            mm.then_inc(G[ph]["pv"], 1)
                            if c + 2 < nc_:
                                turn(c + 2)
                pe.wait_ge(G[ph]["round"], H * NBLK + 1)
                if ph == 1:
                    pe.wait_ge(G[ph]["mask"], 1)
                    for t in range(KT):
                        pe.matmul(outs[0:32, 1, 0:D], share[:, :], v_ctx[:, :, t, 0:HD], start=(t == 0), stop=False)
                    pe.matmul(outs[0:32, 1, 0:D], share[0:H * TAIL, :], v_ctx[0:H * TAIL, :, KT, 0:HD],
                              start=False, stop=True)
                    pe.matmul(outs[0:32, 1, D:D + 1], share[:, :], nan_seen[:, :], start=True, stop=True)\
                        .then_inc(G[ph]["tail"], 1)

            pe.wait_ge(s["consts_made"], N_CONSTS)
            pe.wait_ge(s["fold_made"], 4)
            pe.wait_ge(s["kctx_split"], NCHUNK)
            pe.wait_ge(s["vctx_done"], NCHUNK)
            pe.wait_ge(s["tail_done"], 1)
            pe.wait_ge(s["outs_cleared"], 1)
            pe.wait_ge(s["turned_cleared"], 1)
            pe.wait_ge(s["vself_done"], 2)
            choose(pe, 0, lambda: attention(0), lambda: general(0))

            def project_heads(base, w_sb):
                pe.wait_ge(s["kept_all"], base // 2 + 1)
                for hf in range(NHALF):
                    for c in range(HALF // 32):
                        b = hf * (HALF // 32) + c
                        mm = pe.transpose(bank(hf)[:, 32 * c:32 * c + 32],
                                          heads_out[:, b, :, :].rearrange("p h d -> p (h d)"), ident[0:32, 0:32])
                    mm.then_inc(s["attnT_ps"], 1)
                for hf in range(NHALF):
                    pe.wait_ge(s["attnT_done"], base + hf + 1)
                    for b in range(4):
                        dst = bank(2 + hf)[:, b * D:(b + 1) * D]
                        mm = pe.matmul(dst, attnT[:, hf * HALF + b * P:hf * HALF + (b + 1) * P], w_sb[:, :],
                                       start=True, stop=True)
                    mm.then_inc(s["proj_ps"], 1)

            pe.wait_ge(s["wlate_loaded"], 16 * 9)
            project_heads(0, wos_sb)
            transpose_norm(2)
            for hf in range(NHALF):
                pe.wait_ge(s["normT_done"], 2 + hf + 1)
                pe.matmul(bank(4 + hf), wq_sb[:, :], xnT[:, hf * HALF:(hf + 1) * HALF],
                          start=True, stop=True).then_inc(s["qcross_ps"], 1)
            pe.wait_ge(s["sq_cross"], 2)
            for b in range(NBLK):
                mm = norms(sq_q, b * P, bank(6), b * H)
            mm.then_inc(s["norms_cross"], 1)
            pe.wait_ge(s["cols_done"], 5)
            turn_columns(1)
            pe.wait_ge(s["ktail_made"], 1)
            for hf in range(NHALF):
                pe.wait_ge(s["qcross_split"], hf + 1)
                for i in range(PARTS):
                    for j in range(PARTS):
                        mm = pe.matmul(bank(4 + hf)[0:H * TAIL, :],
                                       ktail_heads[:, i, :, :].rearrange("p h t -> p (h t)"),
                                       qparts[:, j, hf * HALF:(hf + 1) * HALF],
                                       start=(i + j == 0), stop=(i + j == 2 * PARTS - 2))
                mm.then_inc(s["tail_ps"], 1)
            choose(pe, 1, lambda: attention(1), lambda: general(1))
            project_heads(2, wox_sb)
            pe.transpose(bank(5)[:, 0:E * NF], b1_rows[:, :], ident[0:E * NF, 0:E * NF])
            pe.transpose(bank(5)[:, E * NF:E * NF + E], b2_sb[:, :], ident[0:E, 0:E]).then_inc(s["b_ps"], 1)
            transpose_norm(4)
            for hf in range(NHALF):
                pe.wait_ge(s["normT_done"], 4 + hf + 1)
                pe.matmul(bank(6 + hf)[0:E, :], rw_sb[:, :], xnT[:, hf * HALF:(hf + 1) * HALF],
                          start=True, stop=True).then_inc(s["router_ps"], 1)
            pe.wait_ge(s["wffn_loaded"], 32)
            pe.wait_ge(s["b_done"], 1)

            def turn_logits():
                pe.wait_ge(s["logitsT_done"], 2)
                for b in range(NBLK):
                    mm = pe.transpose(bank(5)[:, b * E:(b + 1) * E], logitsT[:, b * P:(b + 1) * P], ident[0:E, 0:E])
                mm.then_inc(s["logits_ps"], 1)

            def turn_gates():
                pe.wait_ge(s["combine_done"], 1)
                for b in range(NBLK):
                    mm = pe.transpose(bank(4 + b // 4)[0:E, b % 4 * P:(b % 4 + 1) * P], combine[:, b, :], ident[:, :])
                    if b % 4 == 3:
                        mm.then_inc(s["combineT_ps"], 1)

            def spread_gate(m):
                if m == 0:
                    pe.wait_ge(s["combineT_done"], 2)
                    pe.wait_ge(s["spread_made"], 1)
                if m >= 2:
                    pe.wait_ge(s["y_scaled"], m - 1)
                hf = m // E
                pe.matmul(bank(4 + m % 2), spread[:, m % E, :], combineT[:, hf * HALF:(hf + 1) * HALF],
                          start=True, stop=True).then_inc(s["cb_ps"], 1)

            def hidden_units(n):
                hf, e, f = n // (E * NF), n // NF % E, n % NF
                if n >= 4:
                    pe.wait_ge(s["hid_relu"], n - 3)
                pe.matmul(bank(n % 4), w1_sb[:, e, f * P:(f + 1) * P], xnT[:, hf * HALF:(hf + 1) * HALF],
                          start=True, stop=True).then_inc(s["hid_ps"], 1)

            def expert_output(n):
                m, f = n // NF, n % NF
                if f == 0:
                    if m >= 2:
                        spread_gate(m)
                    else:
                        pe.wait_ge(s["logitsT_done"], 2)
                pe.wait_ge(s["hid_relu"], n + 1)
                pe.matmul(bank(6 + m % 2), w2_sb[:, m % E, f, :], hidden[:, n % RING, :],
                          start=(f == 0), stop=(f == NF - 1)).then_inc(s["hid_used"], 1)

            for n in range(NHALF * E * NF + LAG):
                if n < NHALF * E * NF:
                    hidden_units(n)
                if n >= LAG:
                    expert_output(n - LAG)
                if n == 1:
                    turn_logits()
                elif n == 5:
                    turn_gates()
                elif n == 7:
                    spread_gate(0)
                    spread_gate(1)
            for hf in range(NHALF):
                pe.wait_ge(s["yT_done"], hf + 1)
                for b in range(4):
                    mm = pe.transpose(bank(hf)[:, b * P:(b + 1) * P], yT[:, hf, b * P:(b + 1) * P], ident[:, :])
                mm.then_inc(s["y_ps"], 1)


_NAMES = ["x", "ctx_768", "L0_attn_Wqvk", "L0_attn_Wo", "L0_xattn_Wq", "L0_xattn_bq", "L0_xattn_Wk", "L0_xattn_bk",
          "L0_xattn_Wv", "L0_xattn_bv", "L0_xattn_Wo", "L0_xattn_bo", "L0_ffn_router_w", "L0_ffn_router_b",
          "L0_ffn_W1", "L0_ffn_b1", "L0_ffn_W2", "L0_ffn_b2"]


def kernel(**inputs):
    import numpy as np
    import concourse.bacc as bacc
    from concourse.bass_utils import run_bass_kernel_spmd as run

    nc = bacc.Bacc("TRN2", target_bir_lowering=False, num_devices=1)
    arrays, args = {}, []
    for name in _NAMES:
        a = np.ascontiguousarray(inputs[name])
        arrays[f"in_{name}"] = a
        args.append(nc.dram_tensor(f"in_{name}", a.shape, mybir.dt.from_np(a.dtype), kind="ExternalInput").ap())
    out = nc.dram_tensor("out", (1, SEQ, D), F32, kind="ExternalOutput").ap()
    decoder_layer(nc, *args, out)
    r = run(nc, [arrays], core_ids=[0])
    return r.results[0]["out"]
```
